# Optimizing a Trainium2 kernel written in Bass

```python
import numpy as np
import jax
import jax.numpy as jnp

def _softmax(x, axis=-1):
    return jax.nn.softmax(x, axis=axis)

def _gelu(x):
    return jax.nn.gelu(x, approximate=True)

def _silu(x):
    return jax.nn.silu(x)

def _sigmoid(x):
    return jax.nn.sigmoid(x)

def _layernorm(x, axis=-1, eps=1e-05):
    m = jnp.mean(x, axis=axis, keepdims=True)
    v = jnp.var(x, axis=axis, keepdims=True)
    return (x - m) / jnp.sqrt(v + eps)

def _scatter_add(tgt, idx, src, axis=0):
    return tgt.at[idx].add(src)

def _segment_sum(src, seg, n):
    return jax.ops.segment_sum(src, seg, n)
kernel_name = 'mk_adj_ffn_d1_adj_r2_da52c5'

def setup_inputs(seed: int=0):
    np.random.seed(seed)
    _w = jnp.asarray

    def _rec_inputs():
        import jax
        import jax.numpy as jnp
        _gk = jax.random.key(seed)
        x = -0.0005207 + 1.001 * jax.random.normal(jax.random.fold_in(_gk, 1), (8192, 128), jnp.float32)
        _a = jax.random.bernoulli(jax.random.fold_in(_gk, 2), 0.00195312, (8192, 8192))
        adj = _a.astype(jnp.int32)
        return (x, adj)
    x, adj = _rec_inputs()

    def _L0_gnn_setup():
        import jax, jax.numpy as jnp
        import numpy as np
        N = 4096
        D_IN = 128
        D_OUT = 128
        NEG_INF = -9000000000000000.0
        key = jax.random.key(seed)
        k1, k2, k3, k4 = jax.random.split(key, 4)
        node_features = jax.random.normal(k1, (N, D_IN), dtype=jnp.float32)
        adjacency_matrix = jax.random.randint(k2, (N, N), 0, 2, dtype=jnp.int32)
        W = jax.random.normal(k3, (D_OUT, D_IN), dtype=jnp.float32) / np.sqrt(D_IN)
        b_W = jnp.zeros((D_OUT,), dtype=jnp.float32)
        a_vec = jax.random.normal(k4, (2 * D_OUT,), dtype=jnp.float32) / np.sqrt(2 * D_OUT)
        b_a = jnp.zeros((1,), dtype=jnp.float32)
        return {'node_features': node_features, 'adjacency_matrix': adjacency_matrix, 'W': W, 'b_W': b_W, 'a_vec': a_vec, 'b_a': b_a}
    _L0_gnn_all = _L0_gnn_setup()
    _L0_gnn_in = {k: v for k, v in _L0_gnn_all.items() if k in ('W', 'b_W', 'a_vec', 'b_a')}
    del _L0_gnn_all

    def _L0_ffn_setup():
        import jax, jax.numpy as jnp
        import numpy as np
        D_MODEL = 128
        N_EXPERTS = 16
        HIDDEN = 256
        SCALE = 0.02
        key = jax.random.key(seed)
        ks = jax.random.split(key, 5)
        x = jax.random.normal(ks[0], (4, 4096, D_MODEL), dtype=jnp.float32)
        gate_w = jax.random.normal(ks[1], (D_MODEL, N_EXPERTS), dtype=jnp.float32) * SCALE
        gate_b = jnp.zeros((N_EXPERTS,), dtype=jnp.float32)
        w1 = jax.random.normal(ks[2], (N_EXPERTS, D_MODEL, HIDDEN), dtype=jnp.float32) * SCALE
        w2 = jax.random.normal(ks[3], (N_EXPERTS, D_MODEL, HIDDEN), dtype=jnp.float32) * SCALE
        w3 = jax.random.normal(ks[4], (N_EXPERTS, HIDDEN, D_MODEL), dtype=jnp.float32) * SCALE
        return {'x': x, 'gate_w': gate_w, 'gate_b': gate_b, 'w1': w1, 'w2': w2, 'w3': w3}
    _L0_ffn_all = _L0_ffn_setup()
    _L0_ffn_in = {k: v for k, v in _L0_ffn_all.items() if k in ('gate_w', 'gate_b', 'w1', 'w2', 'w3')}
    del _L0_ffn_all
    return {'x': x, 'adj': adj, 'L0_gnn_W': _L0_gnn_in['W'], 'L0_gnn_b_W': _L0_gnn_in['b_W'], 'L0_gnn_a_vec': _L0_gnn_in['a_vec'], 'L0_gnn_b_a': _L0_gnn_in['b_a'], 'L0_ffn_gate_w': _L0_ffn_in['gate_w'], 'L0_ffn_gate_b': _L0_ffn_in['gate_b'], 'L0_ffn_w1': _L0_ffn_in['w1'], 'L0_ffn_w2': _L0_ffn_in['w2'], 'L0_ffn_w3': _L0_ffn_in['w3']}

def reference(x, adj, L0_gnn_W, L0_gnn_b_W, L0_gnn_a_vec, L0_gnn_b_a, L0_ffn_gate_w, L0_ffn_gate_b, L0_ffn_w1, L0_ffn_w2, L0_ffn_w3):
    import jax
    import jax.numpy as jnp

    def _L0_gnn_ref(node_features, adjacency_matrix, W, b_W, a_vec, b_a):
        import jax, jax.numpy as jnp
        import numpy as np
        N = 4096
        D_IN = 128
        D_OUT = 128
        NEG_INF = -9000000000000000.0
        h = node_features @ W.T + b_W
        a1, a2 = (a_vec[:D_OUT], a_vec[D_OUT:])
        e = (h @ a1)[:, None] + (h @ a2)[None, :] + b_a[0]
        e = jnp.where(e > 0, e, 0.2 * e)
        scores = jnp.where(adjacency_matrix > 0, e, jnp.float32(NEG_INF))
        attention = jax.nn.softmax(scores, axis=1)
        h_prime = attention @ h
        return h_prime

    def _L0_ffn_ref(x, gate_w, gate_b, w1, w2, w3):
        import jax, jax.numpy as jnp
        import numpy as np
        D_MODEL = 128
        N_EXPERTS = 16
        HIDDEN = 256
        SCALE = 0.02
        n_experts = w1.shape[0]
        logits = jnp.einsum('bsd,de->bse', x, gate_w) + gate_b
        probs = jax.nn.softmax(logits, axis=-1)
        top_probs, top_idx = jax.lax.top_k(probs, 2)
        top_probs = top_probs / jnp.sum(top_probs, axis=-1, keepdims=True)
        dispatch = jnp.sum(jax.nn.one_hot(top_idx, n_experts, dtype=x.dtype) * top_probs[..., None], axis=-2)
        h1 = jnp.einsum('bsd,edh->bseh', x, w1)
        h2 = jnp.einsum('bsd,edh->bseh', x, w2)
        hidden = jax.nn.silu(h1) * h2
        expert_out = jnp.einsum('bseh,eho->bseo', hidden, w3)
        return jnp.einsum('bseo,bse->bso', expert_out, dispatch)
    x = x + _L0_gnn_ref(_layernorm(x, axis=-1), adj, L0_gnn_W, L0_gnn_b_W, L0_gnn_a_vec, L0_gnn_b_a)
    x = x + _L0_ffn_ref(_layernorm(x, axis=-1)[None], L0_ffn_gate_w, L0_ffn_gate_b, L0_ffn_w1, L0_ffn_w2, L0_ffn_w3)[0]
    return x

_drawn_inputs = setup_inputs


def setup_inputs(seed=0):
    import zlib

    import numpy as np

    out = dict(_drawn_inputs(seed))
    spreads = {'L0_gnn_b_W': (0.0, 0.1), 'L0_ffn_gate_b': (0.0, 0.8)}
    factors = {'L0_ffn_gate_w': 8.0, 'L0_ffn_w1': 8.0, 'L0_ffn_w2': 8.0, 'L0_ffn_w3': 8.0}
    for name, (base, spread) in spreads.items():
        noise = np.random.default_rng([zlib.crc32(name.encode()), seed]).standard_normal(out[name].shape)
        drawn = base * np.exp(spread * noise) if base else spread * noise
        out[name] = jnp.asarray(drawn.astype(out[name].dtype))
    for name, factor in factors.items():
        out[name] = (out[name] * factor).astype(out[name].dtype)
    return out
```

```python
from contextlib import ExitStack

import concourse.bass as bass
from concourse import mybir

F32 = mybir.dt.float32
BF16 = mybir.dt.bfloat16
I32 = mybir.dt.int32
U32 = mybir.dt.uint32
ALU = mybir.AluOpType
ACT = mybir.ActivationFunctionType
AX = mybir.AxisListType

P = 128
EPS = 1e-5
BIG = 1e28
LEAK = 0.2
RISE = 1.0 - LEAK


def graph_moe_layer(nc, x, adj, W, b_W, a_vec, b_a, gate_w, gate_b, w1, w2, w3, out):
    N, D = x.shape
    E, _, HID = w1.shape
    NT = N // P
    TPB = 4
    BLK = TPB * P
    NB = N // BLK
    CH = 2048
    CPT = N // CH
    CPB = CPT * TPB
    PC = 1024
    PPT = N // PC
    AHEAD = 3
    PR = 4
    GT = 4
    NG = NT // GT
    ST = 2 * N // P + E
    HC = HID // P
    SU = 4
    GR = 8

    xmid_d = nc.dram_tensor("xmid_d", (N, D), F32, kind="Internal").ap()
    s1_d = nc.dram_tensor("s1_d", (1, N), F32, kind="Internal").ap()
    s2_d = nc.dram_tensor("s2_d", (1, N), BF16, kind="Internal").ap()
    slots_d = nc.dram_tensor("slots_d", (ST * P, D), F32, kind="Internal").ap()
    res_d = nc.dram_tensor("res_d", (ST * P, D), F32, kind="Internal").ap()

    with ExitStack() as ctx:
        def sb(name, shape, dt=F32):
            return ctx.enter_context(nc.sbuf_tensor(name, shape, dt))

        def sem(name):
            return ctx.enter_context(nc.semaphore(name))

        bank = [ctx.enter_context(nc.psum_tensor(f"bank{i}", [P, 512], F32)) for i in range(8)]

        big = sb("big", [P, 2 * TPB * N], BF16)
        maskn = [[big[:, (q * TPB + k) * N:(q * TPB + k + 1) * N] for k in range(TPB)] for q in range(2)]
        half = [big[:, q * TPB * N:(q + 1) * TPB * N].bitcast(F32) for q in range(2)]
        X = sb("X", [P, NT, D])
        s2row = sb("s2row", [P, N], BF16)
        stage = sb("stage", [P, 2, CH], I32)
        s1row = sb("s1row", [P, 2, BLK])
        probs = sb("probs", [P, PR, BLK])
        junk = sb("junk", [P, PC], BF16)
        numT = sb("numT", [P, BLK])
        xres = sb("xres", [P, TPB, D])
        ident = sb("ident", [P, P], BF16)
        identf = sb("identf", [P, P])
        Wx = sb("Wx", [P, D + 1])
        mean_row = sb("mean_row", [P, D + 1])
        scol = sb("scol", [P, NT, 2])
        ns2 = sb("ns2", [P, NT])
        s1cur = sb("s1cur", [P, 2, TPB])
        part = sb("part", [P, TPB, PPT])
        rmax = sb("rmax", [P, TPB])
        amax = sb("amax", [P, TPB])
        mval = sb("mval", [P, 2, TPB])
        noedge = sb("noedge", [P, TPB])
        rden = sb("rden", [P, TPB])
        st = sb("st", [P, GT, 6])
        mv = sb("mv", [P, 2, GT, 2])
        ve = sb("ve", [P, 2, GT])
        sd = sb("sd", [P, 2, GT])
        nr = sb("nr", [P, 4, GT])
        xsum = sb("xsum", [P, 1])
        bigc = sb("bigc", [P, 1])
        onescol = sb("onescol", [P, 1])
        carrier = sb("carrier", [P, 1])
        pcarrier = sb("pcarrier", [P, 2])
        wlast = sb("wlast", [P, 1])
        yb = sb("yb", [P, TPB, D + 1])

        def carve(region, at, *shape):
            n = 1
            for s in shape:
                n *= s
            v = region[:, at:at + n]
            if len(shape) == 2:
                v = v.rearrange("p (a b) -> p a b", a=shape[0])
            return v, at + n

        at = 0
        XN0, at = carve(half[1], at, 2, GT * D)
        xT0, at = carve(half[1], at, 2, GT * D)
        rows0, at = carve(half[1], at, 2, GT * P)
        Wn, at = carve(half[1], at, D)
        acol, at = carve(half[1], at, 2)
        bcol, at = carve(half[1], at, 1)
        ba, at = carve(half[1], at, 1)
        V, at = carve(half[1], at, 2)
        xsrep, at = carve(half[1], at, P)
        rowsb0, at = carve(half[1], at, 2, GT * P // 2)
        rowsb0 = rowsb0.bitcast(BF16)

        at = 0
        w12, at = carve(half[0], at, E, 2 * HID)
        w3s, at = carve(half[0], at, E, HC * D)
        XN1, at = carve(half[0], at, 2, GT * D)
        xT1, at = carve(half[0], at, 2, GT * D)
        gw, at = carve(half[0], at, E)
        gb, at = carve(half[0], at, E)
        ones1, at = carve(half[0], at, P)
        lg, at = carve(half[0], at, 2, GT * E)
        top, at = carve(half[0], at, 2, GT * 8)
        topi, at = carve(half[0], at, 2, GT * 8)
        topi = topi.bitcast(U32)
        tri, at = carve(half[0], at, P // 2)
        tri = tri.bitcast(BF16)
        allone, at = carve(half[0], at, P // 2)
        allone = allone.bitcast(BF16)
        iota_e, at = carve(half[0], at, E)
        iota_t, at = carve(half[0], at, ST)
        assert at <= TPB * N // 2
        at = 0
        xm, at = carve(half[1], at, NT, D)
        route = at
        TE = NT * E
        oh1, at = carve(half[1], at, TE)
        oh2, at = carve(half[1], at, TE)
        cnt, at = carve(half[1], at, TE)
        run, at = carve(half[1], at, TE)
        pos, at = carve(half[1], at, TE)
        tmp, at = carve(half[1], at, TE)
        ohb, at = carve(half[1], at, TE // 2)
        ohb = ohb.bitcast(BF16)
        seg, at = carve(half[1], at, TE)
        assert at <= TPB * N // 2
        cmpt = half[1][:, route:route + ST * E]
        gat, _ = carve(half[1], route, 2 * GR, D)
        jf = s2row[:, :].bitcast(F32)
        at = 0
        l12, at = carve(jf, at, 2, NT)
        i12, at = carve(jf, at, 2, NT)
        wts, at = carve(jf, at, 2, NT)
        slot, at = carve(jf, at, 2, NT)
        sloti, at = carve(jf, at, 2, NT)
        sloti = sloti.bitcast(U32)
        ec, at = carve(jf, at, E)
        et, at = carve(jf, at, E)
        eti, at = carve(jf, at, E)
        eti = eti.bitcast(I32)
        ecum, at = carve(jf, at, E)
        ebase, at = carve(jf, at, E)
        eone, at = carve(jf, at, E)
        tex, at = carve(jf, at, ST)
        texi, at = carve(jf, at, ST)
        texi = texi.bitcast(I32)
        zero, at = carve(jf, at, 9 * D)
        xs, at = carve(jf, at, SU, D)
        assert at <= N // 2
        stf = stage[:, :, :].rearrange("p a b -> p (a b)").bitcast(F32)
        xsT, at = carve(stf, 0, 2, D)
        hidT, at = carve(stf, at, 2, HID)
        ys, at = carve(stf, at, SU, D)
        prf = probs[:, :, :].rearrange("p a b -> p (a b)")
        silu, at = carve(prf, 0, 2, HID)
        hid, at = carve(prf, at, 2, HID)

        w_in = sem("w_in")
        x_in = sem("x_in")
        const_done = sem("const_done")
        pre = sem("pre")
        pe_pre = sem("pe_pre")
        var_ready = sem("var_ready")
        sd_ready = sem("sd_ready")
        ln_chain = sem("ln_chain")
        xn_ready = sem("xn_ready")
        xn_kept = sem("xn_kept")
        xt_done = sem("xt_done")
        xt_ready = sem("xt_ready")
        lin_done = sem("lin_done")
        lin_read = sem("lin_read")
        rows_ready = sem("rows_ready")
        rows_out = [sem("rows_out0"), sem("rows_out1")]
        s2_in = sem("s2_in")
        mean_ready = sem("mean_ready")
        mean_read = sem("mean_read")
        adj_in = [sem("adj_in0"), sem("adj_in1")]
        s1_in = [sem("s1_in0"), sem("s1_in1")]
        nonedge_done = sem("nonedge_done")
        piece_done = sem("piece_done")
        vmax = sem("vmax")
        mval_ready = sem("mval_ready")
        mask_ready = sem("mask_ready")
        trans_done = sem("trans_done")
        logit_ready = sem("logit_ready")
        probs_ready = sem("probs_ready")
        prod_done = sem("prod_done")
        num_ready = sem("num_ready")
        proj_done = sem("proj_done")
        xres_in = sem("xres_in")
        fin = sem("fin")
        xmid_ready = sem("xmid_ready")
        xmid_out = sem("xmid_out")
        zero_ready = sem("zero_ready")
        slots_zero = sem("slots_zero")
        we_in = sem("we_in")
        xm_in = sem("xm_in")
        gconst = sem("gconst")
        rt = sem("rt")
        oh_ready = sem("oh_ready")
        cnt_done = sem("cnt_done")
        ed_ready = sem("ed_ready")
        ee_ready = sem("ee_ready")
        slot_ready = sem("slot_ready")
        tex_ready = sem("tex_ready")
        scattered = sem("scattered")
        xs_in = [sem(f"xs_in{i}") for i in range(SU)]
        xsT_done = sem("xsT_done")
        xsT_ready = sem("xsT_ready")
        h_done = sem("h_done")
        silu_ready = sem("silu_ready")
        hid_ready = sem("hid_ready")
        hT_done = sem("hT_done")
        hT_ready = sem("hT_ready")
        y_done = sem("y_done")
        y_ready = sem("y_ready")
        y_out = [sem(f"y_out{i}") for i in range(SU)]
        gathered = [sem(f"gathered{i}") for i in range(GR)]
        comb1 = sem("comb1")
        comb2 = sem("comb2")
        out_done = sem("out_done")

        maskT = [bank[0], bank[1]]
        logit = [bank[2], bank[3]]
        acc = [bank[4], bank[5]]
        proj = [bank[6], bank[7]]
        tp_bf = [b[:, :].bitcast(BF16)[:, 0:BLK] for b in maskT]

        x_t = x.rearrange("(t p) d -> p t d", p=P)
        xmid_t = xmid_d.rearrange("(t p) d -> p t d", p=P)
        out_t = out.rearrange("(t p) d -> p t d", p=P)

        block = ctx.enter_context(nc.Block())

        @block.sync
        def _(sp):
            sp.dma_start(Wn, W).then_inc(w_in, 16)
            sp.dma_start(acol, a_vec.rearrange("(k o) -> o k", o=D), allow_slow_non_contiguous=True).then_inc(w_in, 16)
            sp.dma_start(bcol, b_W.rearrange("(o a) -> o a", a=1)).then_inc(w_in, 16)
            for c in range(4):
                n = NT // 4
                sp.dma_start(X[:, c * n:(c + 1) * n, :], x_t[:, c * n:(c + 1) * n, :]).then_inc(x_in, 16)
            sp.wait_ge(const_done, 1)
            sp.dma_start(ba[P - 1:P, :], b_a.rearrange("(o a) -> o a", a=1)).then_inc(w_in, 16)

            def load_chunk(b, m):
                k, c = m // CPT, m % CPT
                if not (isinstance(b, int) and b == 0 and m < 2):
                    sp.wait_ge(nonedge_done, b * CPB + m - 1)
                sp.dma_start(stage[:, m % 2, :], adj[bass.ds((b * TPB + k) * P, P), c * CH:(c + 1) * CH]
                             ).then_inc(adj_in[m % 2], 16)

            def load_chunks(b, more):
                for m in range(2, CPB):
                    load_chunk(b, m)
                if more:
                    for m in range(2):
                        load_chunk(b + 1, m)

            def load_s1(b, q):
                sp.dma_start(s1row[:, q, :], s1_d[0:1, bass.ds(b * BLK, BLK)].partition_broadcast(P)
                             ).then_inc(s1_in[q], 16)

            def store_xmid(b):
                sp.wait_ge(xmid_ready, b + 1)
                sp.dma_start(xmid_t[:, bass.ds(b * TPB, TPB), :], xres[:, :, :]).then_inc(xmid_out, 16)

            for m in range(2):
                load_chunk(0, m)
            with sp.Fori(0, NG // 2) as i:
                for u in range(2):
                    sp.wait_ge(rows_ready, 2 * i + u + 1)
                    sp.dma_start(s1_d[0:1, bass.ds((2 * i + u) * GT * P, GT * P)], rows0[0:1, u, :]
                                 ).then_inc(rows_out[u], 16)
                    sp.dma_start(s2_d[0:1, bass.ds((2 * i + u) * GT * P, GT * P)], rowsb0[1:2, u, :]
                                 ).then_inc(rows_out[u], 16)
            for u in range(2):
                sp.wait_ge(rows_out[u], 32 * (NG // 2))
            sp.dma_start(s2row[:, :], s2_d[0:1, :].partition_broadcast(P)).then_inc(s2_in, 16)
            for q in range(2):
                load_s1(q, q)
            load_chunks(0, True)

            def next_s1(b, q):
                sp.wait_ge(logit_ready, NT * (b + 1))
                load_s1(b + 2, q)

            load_chunks(1, True)
            next_s1(0, 0)
            with sp.Fori(0, (NB - 4) // 2) as i:
                for q in range(2):
                    b = 2 * i + 1 + q
                    load_chunks(b + 1, True)
                    store_xmid(b - 1)
                    next_s1(b, 1 - q)
            load_chunks(NB - 2, True)
            store_xmid(NB - 4)
            next_s1(NB - 3, 1)
            load_chunks(NB - 1, False)
            store_xmid(NB - 3)
            sp.wait_ge(trans_done, NT * (NB - 1))
            w12v = w12.rearrange("p e (k h) -> p e k h", k=2)
            sp.dma_start(w12v[:, :, 0, :], w1.rearrange("e d h -> d e h")).then_inc(we_in, 16)
            sp.dma_start(w12v[:, :, 1, :], w2.rearrange("e d h -> d e h")).then_inc(we_in, 16)
            for c in range(HC):
                sp.dma_start(w3s[:, :, c * D:(c + 1) * D],
                             w3[:, c * P:(c + 1) * P, :].rearrange("e h o -> h e o")).then_inc(we_in, 16)
            sp.dma_start(gw, gate_w).then_inc(we_in, 16)
            sp.dma_start(gb[0:1, :], gate_b.rearrange("(a e) -> a e", a=1)).then_inc(we_in, 16)
            store_xmid(NB - 2)
            store_xmid(NB - 1)
            sp.wait_ge(xmid_out, 16 * NB)
            sp.wait_ge(trans_done, NT * NB)
            for c in range(4):
                n = NT // 4
                sp.dma_start(xm[:, c * n:(c + 1) * n, :], xmid_t[:, c * n:(c + 1) * n, :]).then_inc(xm_in, 16)

            sp.wait_ge(scattered, 16 * 2 * NT)

            def load_slots(i, u, first):
                if not first:
                    sp.wait_ge(xsT_done, i - SU + 1)
                sp.dma_start(xs[:, u, :], slots_d[bass.ds(i * P, P), :]).then_inc(xs_in[u], 16)

            for i in range(SU):
                load_slots(i, i, True)
            with sp.Fori(0, ST // SU - 1) as g:
                for u in range(SU):
                    load_slots(SU * (g + 1) + u, u, False)
            with sp.Fori(0, NT // 4) as g:
                sp.wait_ge(comb2, 4 * g + 4)
                sp.dma_start(out_t[:, bass.ds(4 * g, 4), :], xm[:, bass.ds(4 * g, 4), :]).then_inc(out_done, 16)
            sp.wait_ge(out_done, 16 * (NT // 4))

        @block.gpsimd
        def _(pool):
            pool.memset(pcarrier[:, :], 0.0)
            pool.memset(ba, 0.0).then_inc(const_done, 1)
            pool.memset(ident[:, :], 0.0).then_inc(const_done, 1)
            pool.memset(identf[:, :], 0.0).then_inc(const_done, 1)
            pool.wait_ge(const_done, 3)
            for m in (ident, identf):
                pool.affine_select(out=m[:, :], in_=m[:, :], compare_op=ALU.not_equal, fill=1.0, base=0,
                                   pattern=[[-1, P]], channel_multiplier=1).then_inc(const_done, 1)
            pool.memset(Wx[:, D:D + 1], 0.0).then_inc(const_done, 1)
            pool.wait_ge(const_done, 6)
            pool.affine_select(out=Wx[:, D:D + 1], in_=Wx[:, D:D + 1], compare_op=ALU.not_equal, fill=1.0,
                               base=-(P - 1), pattern=[[0, 1]], channel_multiplier=1).then_inc(const_done, 1)
            for u in range(2):
                pool.memset(XN0[:, u, :].rearrange("p (k d) -> p k d", d=D)[:, :, D - 1:D], 1.0
                            ).then_inc(const_done, 1)

            def make_masks(b, q):
                for k in range(TPB):
                    if not (isinstance(b, int) and b == k == 0):
                        pool.wait_ge(mask_ready, b * TPB + k)
                    pool.wait_ge(mval_ready, b * TPB + k + 1)
                    pool.tensor_tensor(pcarrier[:, 1:2], pcarrier[:, 0:1], pcarrier[:, 0:1], ALU.add)
                    pool.tensor_scalar(maskn[q][k], maskn[q][k], -1.0, mval[:, q, k:k + 1],
                                       ALU.mult, ALU.add).then_inc(mask_ready, 1)

            def load_xres(b, first=False):
                if not first:
                    pool.wait_ge(xmid_out, 16 * b)
                pool.dma_start(xres[:, :, :], x_t[:, bass.ds(b * TPB, TPB), :]).then_inc(xres_in, 16)

            make_masks(0, 0)
            load_xres(0, True)
            make_masks(1, 1)
            with pool.Fori(0, (NB - 2) // 2) as i:
                for q in range(2):
                    b = 2 * i + 1 + q
                    make_masks(b + 1, q)
                    load_xres(b)
            load_xres(NB - 1)

            pool.wait_ge(trans_done, NT * (NB - 1))
            pool.memset(ones1[0:1, :], 1.0).then_inc(gconst, 1)
            pool.memset(tri, 1.0).then_inc(gconst, 1)
            pool.memset(allone, 1.0).then_inc(gconst, 1)
            pool.iota(iota_e, pattern=[[1, E]], base=0, channel_multiplier=0,
                      allow_small_or_imprecise_dtypes=True).then_inc(gconst, 1)
            pool.iota(iota_t, pattern=[[1, ST]], base=0, channel_multiplier=0,
                      allow_small_or_imprecise_dtypes=True).then_inc(gconst, 1)
            pool.wait_ge(gconst, 2)
            pool.affine_select(out=tri, in_=tri, compare_op=ALU.is_gt, fill=0.0, base=0,
                               pattern=[[1, P]], channel_multiplier=-1).then_inc(gconst, 1)
            pool.wait_ge(mval_ready, NT)
            pool.memset(zero, 0.0).then_inc(zero_ready, 1)
            pool.memset(eone, 1.0).then_inc(gconst, 1)
            pool.wait_ge(zero_ready, 1)
            zr = slots_d.rearrange("(p a r) d -> p a (r d)", p=P, r=9)
            for a in range(ST // 9):
                pool.dma_start(zr[:, a, :], zero).then_inc(slots_zero, 16)
            pool.wait_ge(slots_zero, 16 * (ST // 9))
            pool.wait_ge(xn_kept, 2 * NG)
            pool.wait_ge(slot_ready, 1)
            for t in range(NT):
                for k in range(2):
                    pool.indirect_dma_start(
                        out=slots_d[:, :],
                        out_offset=bass.IndirectOffsetOnAxis(ap=sloti[:, k, t:t + 1], axis=0),
                        in_=X[:, t, :], in_offset=None).then_inc(scattered, 16)
            with pool.Fori(0, ST // SU) as g:
                for u in range(SU):
                    pool.wait_ge(y_ready, SU * g + u + 1)
                    pool.dma_start(res_d[bass.ds((SU * g + u) * P, P), :], ys[:, u, :]).then_inc(y_out[u], 16)
            for u in range(SU):
                pool.wait_ge(y_out[u], 16 * (ST // SU))
            for t in range(NT):
                r = t % GR
                if t >= GR:
                    pool.wait_ge(comb2, t - GR + 1)
                for k in range(2):
                    pool.indirect_dma_start(
                        out=gat[:, 2 * r + k, :], out_offset=None, in_=res_d[:, :],
                        in_offset=bass.IndirectOffsetOnAxis(ap=sloti[:, k, t:t + 1], axis=0)
                    ).then_inc(gathered[r], 16)

        @block.scalar
        def _(act):
            def ln_group(g, u, s, XN, xT):
                n = NG * s + g
                act.wait_ge(var_ready, n + 1)
                act.activation(sd[:, u, :], ve[:, u, :], ACT.Sqrt).then_inc(sd_ready, 1)
                act.wait_ge(xn_ready, n + 1)
                act.activation(X[:, bass.ds(GT * g, GT), :], XN[:, u, :].rearrange("p (k d) -> p k d", d=D),
                               ACT.Copy).then_inc(xn_kept, 1)
                act.wait_ge(xt_done, n + 1)
                if not (s == 0 and isinstance(g, int) and g < 2):
                    act.wait_ge(lin_done, n - 1)
                act.activation(xT[:, u, :], maskT[u][:, :], ACT.Copy).then_inc(xt_ready, 1)

            for g in range(2):
                ln_group(g, g, 0, XN0, xT0)
            with act.Fori(1, NG // 2) as i:
                for u in range(2):
                    ln_group(2 * i + u, u, 0, XN0, xT0)

            def nonedge(b, q, m):
                act.wait_ge(adj_in[m % 2], 8 * (b * CPB + m - m % 2) + 16)
                k, c = m // CPT, m % CPT
                if m == 0 and not (isinstance(b, int) and b < 2):
                    act.wait_ge(trans_done, NT * (b - 1))
                act.activation(maskn[q][k][:, c * CH:(c + 1) * CH], stage[:, m % 2, :], ACT.Relu,
                               bias=bigc[:, 0:1], scale=-BIG).then_inc(nonedge_done, 1)

            act.wait_ge(pre, 1)
            for m in range(CPB):
                nonedge(0, 0, m)

            def exps(b, j, q, first=False):
                n = NT * b + j
                act.wait_ge(logit_ready, n + 1)
                if not (first and j < PR):
                    act.wait_ge(prod_done, n - PR + 1)
                act.activation(probs[:, j % PR, :], logit[j % 2][:, :], ACT.Exp, bias=scol[:, j, 1:2],
                               scale=RISE).then_inc(probs_ready, 1)

            def numerators(b, q, first=False):
                act.wait_ge(prod_done, NT * (b + 1))
                if not first:
                    act.wait_ge(proj_done, b)
                act.activation(numT[:, :], acc[q][:, :], ACT.Copy).then_inc(num_ready, 1)

            def run_block(b, q, first=False, last=False, second=False):
                for j in range(NT):
                    exps(b, j, q, first)
                    if not last and j % 3 == 0 and j // 3 < CPB:
                        nonedge(b + 1, 1 - q, j // 3)
                    if j == 4 and not first:
                        numerators(b - 1, 1 - q, second)

            run_block(0, 0, first=True)
            run_block(1, 1, second=True)
            with act.Fori(1, NB // 2 - 1) as i:
                for q in range(2):
                    run_block(2 * i + q, q)
            run_block(NB - 2, 0)
            run_block(NB - 1, 1, last=True)
            numerators(NB - 1, 1)

            with act.Fori(0, NG // 2) as i:
                for u in range(2):
                    ln_group(2 * i + u, u, 1, XN1, xT1)
            act.wait_ge(ed_ready, 1)
            act.activation(wts[:, 1, :], l12[:, 0, :], ACT.Exp).then_inc(ee_ready, 1)

            def copy_xsT(i, v, first):
                act.wait_ge(xsT_done, i + 1)
                if not first:
                    act.wait_ge(h_done, i - 1)
                act.activation(xsT[:, v, :], bank[v][:, 0:P], ACT.Copy).then_inc(xsT_ready, 1)

            def do_silu(i, v, first):
                act.wait_ge(h_done, i + 1)
                if not first:
                    act.wait_ge(hid_ready, i - 1)
                act.activation(silu[:, v, :], bank[2 + v][:, 0:HID], ACT.Silu).then_inc(silu_ready, 1)

            def copy_y(i, u, first):
                act.wait_ge(y_done, i + 1)
                if not first:
                    act.wait_ge(y_out[u], 16 * (i // SU))
                act.activation(ys[:, u, :], bank[6 + u % 2][:, 0:D], ACT.Copy).then_inc(y_ready, 1)

            def step(i, u, lo, hi, first):
                if hi >= 1:
                    copy_xsT(i + 1, (u + 1) % 2, first and i + 1 < 2)
                if hi >= 0:
                    do_silu(i, u % 2, first and i < 2)
                if lo >= 2:
                    copy_y(i - 2, (u - 2) % SU, first and i - 2 < SU)

            copy_xsT(0, 0, True)
            for i in range(2 * SU):
                step(i, i % SU, i, 9, i < SU + 2)
            with act.Fori(2, ST // SU - 1) as g:
                for u in range(SU):
                    i = SU * g + u
                    copy_xsT(i + 1, (u + 1) % 2, False)
                    do_silu(i, u % 2, False)
                    act.wait_ge(y_done, i - 1)
                    act.wait_ge(y_out[(u - 2) % SU], 16 * (g if u >= 2 else g - 1))
                    act.activation(ys[:, (u - 2) % SU, :], bank[6 + u % 2][:, 0:D], ACT.Copy).then_inc(y_ready, 1)
            for i in range(ST - SU, ST + 2):
                step(i, i % SU, 9, ST - 1 - i, False)

        @block.tensor
        def _(pe):
            pe.wait_ge(const_done, 5)
            pe.wait_ge(pre, 2)
            pe.transpose(bank[0][:, 0:P], Wn, identf[:, :]).then_inc(pe_pre, 1)
            pe.matmul(bank[1][:, 0:2], Wn, acol, start=True, stop=True).then_inc(pe_pre, 1)
            pe.wait_ge(pre, 4)

            def transpose_group(g, u, s, XN, read):
                n = NG * s + g
                pe.wait_ge(xn_ready, n + 1)
                if read:
                    pe.wait_ge(xt_ready, n - 1)
                for k in range(GT):
                    t = pe.transpose(maskT[u][:, k * P:(k + 1) * P], XN[:, u, k * D:(k + 1) * D], identf[:, :])
                t.then_inc(xt_done, 1)

            def group0(g, u, read):
                transpose_group(g, u, 0, XN0, read)
                pe.wait_ge(xt_ready, g + 1)
                if read:
                    pe.wait_ge(lin_read, g - 1)
                pe.matmul(logit[u][0:2, :], V, xT0[:, u, :], start=True, stop=True)
                for k in range(GT):
                    pe.matmul(acc[u][:, 2 * k:2 * k + 2], xT0[:, u, k * P:(k + 1) * P], V, start=True, stop=True)
                for k in range(GT):
                    m = pe.matmul(acc[u][:, 16:17], XN0[:, u, k * D:(k + 1) * D], onescol[:, 0:1],
                                  start=(k == 0), stop=(k == GT - 1))
                m.then_inc(lin_done, 1)

            for g in range(2):
                group0(g, g, False)
            with pe.Fori(1, NG // 2) as i:
                for u in range(2):
                    group0(2 * i + u, u, True)
            pe.wait_ge(mean_ready, 1)
            pe.matmul(proj[0][:, 0:D + 1], xsrep, Wx[:, :], start=True, stop=True).then_inc(pe_pre, 1)

            def transposes(b, j, q, first=False):
                n = NT * b + j
                if j == 0:
                    pe.wait_ge(mask_ready, TPB * (b + 1))
                if not (first and j < 2):
                    pe.wait_ge(logit_ready, n - 1)
                for k in range(TPB):
                    t = pe.transpose(tp_bf[j % 2][:, k * P:(k + 1) * P], maskn[q][k][:, j * P:(j + 1) * P],
                                     ident[:, :])
                t.then_inc(trans_done, 1)

            def product(b, j, q, first=False):
                n = NT * b + j
                pe.wait_ge(probs_ready, n + 1)
                if j == 0 and not first:
                    pe.wait_ge(num_ready, b - 1)
                pe.matmul(acc[q][:, :], X[:, j, :], probs[:, j % PR, :], start=(j == 0), stop=(j == NT - 1)
                          ).then_inc(prod_done, 1)

            def project(b, first=False):
                pe.wait_ge(num_ready, b + 1)
                if first:
                    pe.wait_ge(mean_read, 1)
                else:
                    pe.wait_ge(xmid_ready, b)
                for k in range(TPB):
                    m = pe.matmul(proj[k // 2][:, k % 2 * (D + 1):(k % 2 + 1) * (D + 1)],
                                  numT[:, k * P:(k + 1) * P], Wx[:, :], start=True, stop=True)
                m.then_inc(proj_done, 1)

            def run_block(b, q, first=False, last=False, second=False):
                for j in range(NT):
                    if j + AHEAD < NT:
                        transposes(b, j + AHEAD, q, first)
                    elif not last:
                        transposes(b + 1, j + AHEAD - NT, 1 - q)
                    product(b, j, q, first or second)
                    if j == 8 and not first:
                        project(b - 1, second)

            pe.wait_ge(xt_ready, NG)
            pe.wait_ge(lin_read, NG)
            for j in range(AHEAD):
                transposes(0, j, 0, first=True)
            run_block(0, 0, first=True)
            run_block(1, 1, second=True)
            with pe.Fori(1, NB // 2 - 1) as i:
                for q in range(2):
                    run_block(2 * i + q, q)
            run_block(NB - 2, 0)
            run_block(NB - 1, 1, last=True)
            project(NB - 1)

            pe.wait_ge(we_in, 16 * (4 + HC))
            pe.wait_ge(gconst, 7)
            pe.wait_ge(logit_ready, NT * NB)
            pe.wait_ge(num_ready, NB)

            def group1(g, u):
                transpose_group(g, u, 1, XN1, True)
                pe.wait_ge(xt_ready, NG + g + 1)
                pe.wait_ge(lin_read, NG + g - 1)
                for k in range(GT):
                    pe.matmul(acc[u][:, k * E:(k + 1) * E], xT1[:, u, k * P:(k + 1) * P], gw, start=True, stop=False)
                    m = pe.matmul(acc[u][:, k * E:(k + 1) * E], ones1[0:1, :], gb[0:1, :], start=False, stop=True)
                m.then_inc(lin_done, 1)

            with pe.Fori(0, NG // 2) as i:
                for u in range(2):
                    group1(2 * i + u, u)

            pe.wait_ge(oh_ready, 1)
            for h in range(2):
                pe.matmul(bank[h][:, :], tri, ohb[:, h * 512:(h + 1) * 512], start=True, stop=True)
            for h in range(2):
                m = pe.matmul(bank[2 + h][:, :], allone, ohb[:, h * 512:(h + 1) * 512], start=True, stop=True)
            m.then_inc(cnt_done, 1)
            pe.wait_ge(tex_ready, 1)

            def expert_of(i):
                return pe.value_load(texi[0:1, bass.ds(i, 1)], min_val=0, max_val=E - 1)

            def t_x(i, u, first):
                pe.wait_ge(xs_in[u], 16 * uses(i, u))
                if not first:
                    pe.wait_ge(xsT_ready, i - 1)
                pe.transpose(bank[u % 2][:, 0:P], xs[:, u, :], identf[:, :]).then_inc(xsT_done, 1)

            def m_h(i, u, first):
                e = expert_of(i)
                pe.wait_ge(xsT_ready, i + 1)
                if not first:
                    pe.wait_ge(hid_ready, i - 1)
                pe.matmul(bank[2 + u % 2][:, :], xsT[:, u % 2, :],
                          w12[:, bass.ds(e, 1), :].rearrange("p a b -> p (a b)"), start=True, stop=True
                          ).then_inc(h_done, 1)

            def t_h(i, u, first):
                pe.wait_ge(hid_ready, i + 1)
                if not first:
                    pe.wait_ge(hT_ready, i - 1)
                for c in range(HC):
                    t = pe.transpose(bank[4 + u % 2][:, c * P:(c + 1) * P], hid[:, u % 2, c * P:(c + 1) * P],
                                     identf[:, :])
                t.then_inc(hT_done, 1)

            def m_y(i, u, first):
                e = expert_of(i)
                pe.wait_ge(hT_ready, i + 1)
                if not first:
                    pe.wait_ge(y_ready, i - 1)
                for c in range(HC):
                    m = pe.matmul(bank[6 + u % 2][:, 0:D], hidT[:, u % 2, c * P:(c + 1) * P],
                                  w3s[:, bass.ds(e, 1), c * D:(c + 1) * D].rearrange("p a b -> p (a b)"),
                                  start=(c == 0), stop=(c == HC - 1))
                m.then_inc(y_done, 1)

            def uses(i, u):
                return i // SU + 1 if isinstance(i, int) else round_of

            t_x(0, 0, True)
            for i in range(SU):
                m_h(i, i, i < 2)
                t_x(i + 1, (i + 1) % SU, i + 1 < 2)
                if i >= 1:
                    t_h(i - 1, i - 1, i - 1 < 2)
                if i >= 2:
                    m_y(i - 2, i - 2, i - 2 < 2)
            with pe.Fori(1, ST // SU - 1) as g:
                for u in range(SU):
                    i = SU * g + u
                    m_h(i, u, False)
                    round_of = g + 1 if u + 1 < SU else g + 2
                    t_x(i + 1, (u + 1) % SU, False)
                    t_h(i - 1, (u - 1) % SU, False)
                    m_y(i - 2, (u - 2) % SU, False)
            for i in range(ST - SU, ST + 2):
                if i < ST:
                    m_h(i, i % SU, False)
                if i + 1 < ST:
                    t_x(i + 1, (i + 1) % SU, False)
                if i - 1 < ST:
                    t_h(i - 1, (i - 1) % SU, False)
                m_y(i - 2, (i - 2) % SU, False)

        @block.vector
        def _(dve):
            dve.memset(bigc[:, :], BIG).then_inc(pre, 1)
            dve.memset(onescol[:, :], 1.0)
            dve.memset(xsum[:, :], 0.0)
            dve.wait_ge(w_in, 64)
            dve.tensor_copy(wlast[:, :], Wn[:, D - 1:D]).then_inc(ln_chain, 1)
            dve.wait_ge(ln_chain, 1)
            dve.tensor_scalar(Wn[:, 0:D - 1], Wn[:, 0:D - 1], wlast[:, 0:1], None, ALU.subtract)
            dve.tensor_copy(Wn[:, D - 1:D], bcol).then_inc(pre, 1)
            dve.wait_ge(pe_pre, 2)
            dve.tensor_copy(Wx[:, 0:D], bank[0][:, 0:P]).then_inc(pre, 1)
            dve.tensor_copy(V[:, 1:2], bank[1][:, 1:2])
            dve.tensor_tensor(V[:, 0:1], bank[1][:, 0:1], ba, ALU.add).then_inc(pre, 1)
            PRE = 1
            LINKS = [7, 9]

            def ln_group(s, g, u, XN, src, free, ncol):
                n = NG * s + g
                before = PRE + LINKS[0] * NG * s + LINKS[s] * g
                done = [0]

                def link(ins, carry=False):
                    done[0] += 1
                    ins.then_inc(ln_chain, 1)
                    dve.wait_ge(ln_chain, before + done[0])
                    if carry:
                        dve.memset(carrier[:, :], 0.0)

                for k in range(GT):
                    ins = dve.bn_stats(st[:, k, :], src[:, bass.ds(GT * g + k, 1), :].rearrange("p a d -> p (a d)"))
                link(ins, carry=True)
                for k in range(GT):
                    ins = dve.bn_aggr(mv[:, u, k, :], st[:, k, :])
                link(ins)
                dve.tensor_scalar(ve[:, u, :], mv[:, u, :, 1], EPS, None, ALU.add).then_inc(var_ready, 1)
                dve.wait_ge(sd_ready, n + 1)
                link(dve.reciprocal(nr[:, 0, :], sd[:, u, :]))
                link(dve.tensor_tensor(nr[:, 1, :], nr[:, 0, :], nr[:, 0, :], ALU.mult))
                link(dve.tensor_tensor(nr[:, 2, :], nr[:, 1, :], ve[:, u, :], ALU.mult))
                link(dve.tensor_scalar(nr[:, 3, :], nr[:, 2, :], -0.5, 1.5, ALU.mult, ALU.add))
                link(dve.tensor_tensor(nr[:, 1, :], nr[:, 0, :], nr[:, 3, :], ALU.mult))
                if free:
                    dve.wait_ge(xn_kept, n - 1)
                    dve.wait_ge(lin_done, n - 1)
                for k in range(GT):
                    ins = dve.tensor_scalar(XN[:, u, k * D:k * D + ncol],
                                            src[:, bass.ds(GT * g + k, 1), 0:ncol].rearrange("p a d -> p (a d)"),
                                            mv[:, u, k, 0:1], nr[:, 1, k:k + 1], ALU.subtract, ALU.mult)
                ins.then_inc(xn_ready, 1)
                return link

            def group0(g, u, turn):
                ln_group(0, g, u, XN0, X, turn is not None, D - 1)
                dve.wait_ge(lin_done, g + 1)
                if turn is not None:
                    dve.wait_ge(rows_out[u], 32 * turn)
                dve.tensor_copy(rows0[0:2, u, :], logit[u][0:2, :])
                dve.tensor_copy(rowsb0[0:2, u, :], logit[u][0:2, :]).then_inc(rows_ready, 1)
                dve.tensor_copy(scol[:, bass.ds(GT * g, GT), :],
                                acc[u][:, 0:2 * GT].rearrange("p (k s) -> p k s", s=2))
                if turn is not None:
                    dve.wait_ge(lin_read, g)
                dve.tensor_tensor(xsum[:, :], xsum[:, :], acc[u][:, 16:17], ALU.add).then_inc(lin_read, 1)

            dve.wait_ge(x_in, 64)
            dve.wait_ge(const_done, 9)
            group0(0, 0, None)
            dve.wait_ge(lin_read, 1)
            group0(1, 1, None)
            with dve.Fori(1, NG // 2) as turn:
                for u in range(2):
                    group0(2 * turn + u, u, turn)
            dve.wait_ge(lin_read, NG)
            dve.tensor_copy(xsrep, xsum[:, 0:1].to_broadcast([P, P])).then_inc(mean_ready, 1)
            dve.tensor_scalar(ns2[:, :], scol[:, :, 1], -1.0, None, ALU.mult)
            dve.wait_ge(pe_pre, 3)
            dve.tensor_copy(mean_row[:, :], proj[0][:, 0:D + 1]).then_inc(mean_read, 1)

            VLINKS = 1 + 2 * TPB
            FLINKS = 3

            def piece(b, q, k, c, h):
                if k == c == h == 0:
                    dve.tensor_copy(s1cur[:, q, :], scol[:, bass.ds(TPB * b, TPB), 0]).then_inc(vmax, 1)
                lo = c * CH + h * PC
                dve.tensor_tensor_reduce(junk[:, :], s2row[:, lo:lo + PC], maskn[q][k][:, lo:lo + PC], 1.0, -3e38,
                                         ALU.subtract, ALU.max,
                                         part[:, k, lo // PC:lo // PC + 1]).then_inc(piece_done, 1)
                if lo + PC == N:
                    before = VLINKS * b + 1 + 2 * k
                    dve.wait_ge(piece_done, (b * TPB + k + 1) * PPT)
                    dve.tensor_reduce(rmax[:, k:k + 1], part[:, k, :], AX.X, ALU.max).then_inc(vmax, 1)
                    dve.wait_ge(vmax, before + 1)
                    dve.tensor_scalar(amax[:, k:k + 1], rmax[:, k:k + 1], -1.0, s1cur[:, q, k:k + 1],
                                      ALU.mult, ALU.max).then_inc(vmax, 1)
                    dve.wait_ge(vmax, before + 2)
                    if not (isinstance(b, int) and b < 2):
                        dve.wait_ge(mask_ready, TPB * (b - 2) + k + 1)
                    dve.scalar_tensor_tensor(out=mval[:, q, k:k + 1], in0=rmax[:, k:k + 1], scalar=-1.0 / RISE,
                                             in1=amax[:, k:k + 1], op0=ALU.mult, op1=ALU.subtract
                                             ).then_inc(mval_ready, 1)

            def logits(b, j, q, i, first):
                n = NT * b + j
                if j == 0:
                    dve.wait_ge(s1_in[q], 16 * (i + 1))
                dve.wait_ge(trans_done, n + 1)
                if not (first and j < 2):
                    dve.wait_ge(probs_ready, n - 1)
                dve.scalar_tensor_tensor(out=logit[j % 2][:, :], in0=s1row[:, q, :], scalar=ns2[:, j:j + 1],
                                         in1=tp_bf[j % 2], op0=ALU.max, op1=ALU.add).then_inc(logit_ready, 1)

            def finish(b, part_of):
                before = FLINKS * b
                if part_of == 0:
                    dve.wait_ge(proj_done, b + 1)
                    for h in range(2):
                        ins = dve.tensor_scalar(noedge[:, 2 * h:2 * h + 2], proj[h][:, D:2 * D + 2:D + 1], 0.0, None,
                                                ALU.is_equal)
                    ins.then_inc(fin, 1)
                    dve.wait_ge(fin, before + 1)
                elif part_of <= TPB:
                    k = part_of - 1
                    ins = dve.scalar_tensor_tensor(out=yb[:, k, :], in0=mean_row[:, :], scalar=noedge[:, k:k + 1],
                                                   in1=proj[k // 2][:, k % 2 * (D + 1):(k % 2 + 1) * (D + 1)],
                                                   op0=ALU.mult, op1=ALU.add)
                    if part_of == TPB:
                        ins.then_inc(fin, 1)
                        dve.wait_ge(fin, before + 2)
                elif part_of == TPB + 1:
                    dve.reciprocal(rden[:, :], yb[:, :, D]).then_inc(fin, 1)
                    dve.wait_ge(fin, before + 3)
                    dve.wait_ge(xres_in, 16 * (b + 1))
                else:
                    k = part_of - TPB - 2
                    ins = dve.scalar_tensor_tensor(out=xres[:, k, :], in0=yb[:, k, 0:D], scalar=rden[:, k:k + 1],
                                                   in1=xres[:, k, :], op0=ALU.mult, op1=ALU.add)
                    if k == TPB - 1:
                        ins.then_inc(xmid_ready, 1)

            FPARTS = 2 * TPB + 2

            def run_block(b, q, i, first=False, last=False):
                for j in range(NT):
                    if not last and j % 3 == 1 and j // 3 < CPB:
                        dve.wait_ge(nonedge_done, (b + 1) * CPB + j // 3 + 1)
                    if not last and j % 3 and j // 3 < CPB:
                        dve.wait_ge(piece_done, TPB * PPT * (b + 1) + j // 3 * 2 + j % 3 - 1)
                    logits(b, j, q, i, first)
                    if not last and j % 3 and j // 3 < CPB:
                        piece(b + 1, 1 - q, j // 3 // CPT, j // 3 % CPT, j % 3 - 1)
                    if not first and 0 <= j - 50 < FPARTS:
                        finish(b - 1, j - 50)

            dve.wait_ge(s2_in, 16)
            for m in range(CPB):
                dve.wait_ge(nonedge_done, m + 1)
                for h in range(2):
                    if m or h:
                        dve.wait_ge(piece_done, 2 * m + h)
                    piece(0, 0, m // CPT, m % CPT, h)
            run_block(0, 0, 0, first=True)
            run_block(1, 1, 0)
            with dve.Fori(1, NB // 2 - 1) as i:
                for q in range(2):
                    run_block(2 * i + q, q, i)
            run_block(NB - 2, 0, NB // 2 - 1)
            run_block(NB - 1, 1, NB // 2 - 1, last=True)
            for f in range(FPARTS):
                finish(NB - 1, f)

            dve.wait_ge(trans_done, NT * (NB - 1))
            dve.wait_ge(xm_in, 64)

            def group1(g, u):
                link = ln_group(1, g, u, XN1, xm, True, D)
                dve.wait_ge(lin_done, NG + g + 1)
                dve.tensor_copy(lg[:, u, :], acc[u][:, 0:GT * E]).then_inc(lin_read, 1)
                dve.wait_ge(lin_read, NG + g + 1)
                dve.memset(carrier[:, :], 0.0)
                for k in range(GT):
                    ins = dve.max(top[:, u, 8 * k:8 * k + 8], lg[:, u, k * E:(k + 1) * E])
                link(ins, carry=True)
                for k in range(GT):
                    ins = dve.max_index(topi[:, u, 8 * k:8 * k + 8], top[:, u, 8 * k:8 * k + 8],
                                        lg[:, u, k * E:(k + 1) * E])
                link(ins, carry=True)
                for c in range(2):
                    dve.tensor_copy(l12[:, c, bass.ds(GT * g, GT)], top[:, u, c:GT * 8:8])
                    dve.tensor_copy(i12[:, c, bass.ds(GT * g, GT)], topi[:, u, c:GT * 8:8])

            with dve.Fori(0, NG // 2) as turn:
                for u in range(2):
                    group1(2 * turn + u, u)

            rts = [0]

            def link(ins):
                rts[0] += 1
                ins.then_inc(rt, 1)
                dve.wait_ge(rt, rts[0])

            def by_te(v):
                return v.rearrange("p (t e) -> p t e", e=E)

            def by_et(v):
                return v.rearrange("p (e t) -> p e t", e=E)

            dve.wait_ge(gconst, 7)
            link(dve.memset(seg, 1.0))
            link(dve.memset(by_et(seg)[:, :, 0:1], 0.0))
            dve.tensor_tensor(l12[:, 0, :], l12[:, 1, :], l12[:, 0, :], ALU.subtract).then_inc(ed_ready, 1)
            for c, oh in enumerate((oh1, oh2)):
                link(dve.tensor_tensor(by_te(oh), iota_e.unsqueeze(1).to_broadcast([P, NT, E]),
                                       i12[:, c, :].unsqueeze(2).to_broadcast([P, NT, E]), ALU.is_equal))
            dve.tensor_tensor(ohb, oh1, oh2, ALU.add).then_inc(oh_ready, 1)
            dve.wait_ge(ee_ready, 1)
            link(dve.tensor_scalar(slot[:, 0, :], wts[:, 1, :], 1.0, None, ALU.add))
            link(dve.reciprocal(wts[:, 0, :], slot[:, 0, :]))
            link(dve.tensor_tensor(wts[:, 1, :], wts[:, 1, :], wts[:, 0, :], ALU.mult))
            dve.wait_ge(cnt_done, 1)
            for h in range(2):
                ins = dve.tensor_copy(by_et(cnt)[:, :, h * NT // 2:(h + 1) * NT // 2],
                                      bank[2 + h][:, :].rearrange("p (t e) -> p e t", e=E))
            link(ins)
            link(dve.tensor_tensor_scan(run, seg, cnt, 0.0, ALU.mult, ALU.add))
            link(dve.tensor_copy(ec, by_et(run)[:, :, NT - 1]))
            link(dve.tensor_scalar(eti, ec, 1.0 / P, 0.5 - 0.5 / P, ALU.mult, ALU.add))
            link(dve.tensor_copy(et, eti))
            link(dve.tensor_tensor_scan(ecum, eone, et, 0.0, ALU.mult, ALU.add))
            link(dve.tensor_tensor(ec, ecum, et, ALU.subtract))
            link(dve.tensor_scalar(ebase, ec, float(P), None, ALU.mult))
            link(dve.tensor_tensor(pos, run, cnt, ALU.subtract))
            link(dve.tensor_tensor(by_et(pos), by_et(pos), ebase.unsqueeze(2).to_broadcast([P, E, NT]), ALU.add))
            for h in range(2):
                ins = dve.tensor_tensor(by_te(tmp)[:, h * NT // 2:(h + 1) * NT // 2, :],
                                        pos.rearrange("p (e t) -> p t e", e=E)[:, h * NT // 2:(h + 1) * NT // 2, :],
                                        by_te(bank[h][:, :]), ALU.add)
            link(ins)
            for c, oh in enumerate((oh1, oh2)):
                link(dve.tensor_tensor(oh, oh, tmp, ALU.mult))
                link(dve.tensor_reduce(slot[:, c, :], by_te(oh), AX.X, ALU.add))
            dve.tensor_copy(sloti, slot).then_inc(slot_ready, 1)
            c1 = cmpt[0:1, :].rearrange("p (i e) -> p i e", e=E)
            link(dve.tensor_tensor(c1, iota_t[0:1, :].unsqueeze(2).to_broadcast([1, ST, E]),
                                   ecum[0:1, :].unsqueeze(1).to_broadcast([1, ST, E]), ALU.is_ge))
            link(dve.tensor_reduce(tex[0:1, :], c1, AX.X, ALU.add))
            dve.tensor_scalar(texi[0:1, :], tex[0:1, :], float(E - 1), None, ALU.min).then_inc(tex_ready, 1)

            def do_hid(i, v, first):
                dve.wait_ge(silu_ready, i + 1)
                if not first:
                    dve.wait_ge(hT_done, i - 1)
                dve.tensor_tensor(hid[:, v, :], silu[:, v, :], bank[2 + v][:, HID:2 * HID], ALU.mult
                                  ).then_inc(hid_ready, 1)

            def copy_hT(i, v, first):
                dve.wait_ge(hT_done, i + 1)
                if not first:
                    dve.wait_ge(y_done, i - 1)
                dve.tensor_copy(hidT[:, v, :], bank[4 + v][:, 0:HID]).then_inc(hT_ready, 1)

            do_hid(0, 0, True)
            copy_hT(0, 0, True)
            do_hid(1, 1, True)
            copy_hT(1, 1, True)
            with dve.Fori(1, ST // 2) as g:
                for v in range(2):
                    do_hid(2 * g + v, v, False)
                    copy_hT(2 * g + v, v, False)

            with dve.Fori(0, NT // GR) as g:
                for r in range(GR):
                    t = GR * g + r
                    xt = xm[:, bass.ds(t, 1), :].rearrange("p a d -> p (a d)")
                    dve.wait_ge(gathered[r], 32 * (g + 1))
                    dve.scalar_tensor_tensor(out=xt, in0=gat[:, 2 * r, :], scalar=wts[:, 0, bass.ds(t, 1)], in1=xt,
                                             op0=ALU.mult, op1=ALU.add).then_inc(comb1, 1)
                    dve.wait_ge(comb1, t + 1)
                    dve.scalar_tensor_tensor(out=xt, in0=gat[:, 2 * r + 1, :], scalar=wts[:, 1, bass.ds(t, 1)],
                                             in1=xt, op0=ALU.mult, op1=ALU.add).then_inc(comb2, 1)


_INS = ["x", "adj", "L0_gnn_W", "L0_gnn_b_W", "L0_gnn_a_vec", "L0_gnn_b_a", "L0_ffn_gate_w", "L0_ffn_gate_b",
        "L0_ffn_w1", "L0_ffn_w2", "L0_ffn_w3"]


def kernel(**inputs):
    import numpy as np
    import concourse.bacc as bacc
    from concourse.bass_utils import run_bass_kernel_spmd

    nc = bacc.Bacc("TRN2", target_bir_lowering=False, num_devices=1, dynamic_dma_scratch_size=8192)
    arrays, args = {}, []
    for name in _INS:
        a = np.ascontiguousarray(inputs[name])
        arrays[f"in_{name}"] = a
        args.append(nc.dram_tensor(f"in_{name}", a.shape, mybir.dt.from_np(a.dtype), kind="ExternalInput").ap())
    out = nc.dram_tensor("out", inputs["x"].shape, F32, kind="ExternalOutput").ap()
    graph_moe_layer(nc, *args, out)
    r = run_bass_kernel_spmd(nc, [arrays], core_ids=[0])
    return r.results[0]["out"]
```

```python
from contextlib import ExitStack

import concourse.bass as bass
from concourse import mybir

F32 = mybir.dt.float32
BF16 = mybir.dt.bfloat16
I32 = mybir.dt.int32
U32 = mybir.dt.uint32
ALU = mybir.AluOpType
ACT = mybir.ActivationFunctionType
AX = mybir.AxisListType

P = 128
EPS = 1e-5
BIG = 1e28
LEAK = 0.2
RISE = 1.0 - LEAK


def graph_moe_layer(nc, x, adj, W, b_W, a_vec, b_a, gate_w, gate_b, w1, w2, w3, out):
    N, D = x.shape
    E, _, HID = w1.shape
    NT = N // P
    TPB = 4
    BLK = TPB * P
    NB = N // BLK
    CH = 2048
    CPT = N // CH
    CPB = CPT * TPB
    PC = 1024
    PPT = N // PC
    AHEAD = 3
    PR = 4
    GT = 4
    NG = NT // GT
    ST = 2 * N // P + E
    HC = HID // P
    SU = 4
    GR = 8
    PAIRS = 2 * NT
    JC = 8

    PPC = CH // PC
    PPB = CPB * PPC
    LAG = 3
    NONEDGE_AT = {int(1.86 * i): i for i in range(PPB)}
    PIECE_AT = {j + LAG: (i // PPC, i % PPC) for j, i in NONEDGE_AT.items()}
    ROW_END_AT = {}
    for j, (m, h) in PIECE_AT.items():
        if m % CPT == CPT - 1 and h == PPC - 1:
            k = m // CPT
            if k == TPB - 1:
                ROW_END_AT[j] = (k, (0, 1, 2))
            else:
                for step in range(3):
                    ROW_END_AT[j + 1 + step] = (k, (step,))
    END_AT = [j for j in range(12, NT) if j not in PIECE_AT and j not in ROW_END_AT]

    xmid_d = nc.dram_tensor("xmid_d", (N, D), F32, kind="Internal").ap()
    s1_d = nc.dram_tensor("s1_d", (1, N), F32, kind="Internal").ap()
    s2_d = nc.dram_tensor("s2_d", (1, N), BF16, kind="Internal").ap()
    x2_d = nc.dram_tensor("x2_d", (N, D), F32, kind="Internal").ap()
    res_d = nc.dram_tensor("res_d", (2 * N + ST * P, D), F32, kind="Internal").ap()

    with ExitStack() as ctx:
        def sb(name, shape, dt=F32):
            return ctx.enter_context(nc.sbuf_tensor(name, shape, dt))

        def sem(name):
            return ctx.enter_context(nc.semaphore(name))

        bank = [ctx.enter_context(nc.psum_tensor(f"bank{i}", [P, 512], F32)) for i in range(8)]

        big = sb("big", [P, 2 * TPB * N], BF16)
        maskn = [[big[:, (q * TPB + k) * N:(q * TPB + k + 1) * N] for k in range(TPB)] for q in range(2)]
        half = [big[:, q * TPB * N:(q + 1) * TPB * N].bitcast(F32) for q in range(2)]
        X = sb("X", [P, NT, D])
        s2row = sb("s2row", [P, N], BF16)
        stage = sb("stage", [P, 2, CH], I32)
        s1row = sb("s1row", [P, 2, BLK])
        probs = sb("probs", [P, PR, BLK])
        scrap = sb("scrap", [P, 2, PC], BF16)
        numT = sb("numT", [P, BLK])
        xres = sb("xres", [P, TPB, D])
        ident = sb("ident", [P, P], BF16)
        identf = sb("identf", [P, P])
        Wx = sb("Wx", [P, D + 1])
        mean_row = sb("mean_row", [P, D + 1])
        scol = sb("scol", [P, NT, 2])
        ns2 = sb("ns2", [P, NT])
        s1cur = sb("s1cur", [P, 2, TPB])
        part = sb("part", [P, TPB, PPT])
        rmax = sb("rmax", [P, TPB])
        amax = sb("amax", [P, TPB])
        mval = sb("mval", [P, 2, TPB])
        noedge = sb("noedge", [P, TPB])
        rden = sb("rden", [P, TPB])
        bigc = sb("bigc", [P, 1])
        onescol = sb("onescol", [P, 1])
        pcarrier = sb("pcarrier", [P, 2])
        wlast = sb("wlast", [P, 1])
        den = sb("den", [P, TPB])
        nshare = sb("nshare", [P, TPB])

        def carve(region, at, *shape):
            n = 1
            for s in shape:
                n *= s
            v = region[:, at:at + n]
            if len(shape) == 2:
                v = v.rearrange("p (a b) -> p a b", a=shape[0])
            return v, at + n

        at = 0
        XN0, at = carve(half[1], at, 2, GT * D)
        xT0, at = carve(half[1], at, 2, GT * D)
        rows0, at = carve(half[1], at, 2, GT * P)
        Wn, at = carve(half[1], at, D)
        acol, at = carve(half[1], at, 2)
        bcol, at = carve(half[1], at, 1)
        ba, at = carve(half[1], at, 1)
        V, at = carve(half[1], at, 2)
        xsrep, at = carve(half[1], at, P)
        xsum, at = carve(half[1], at, D)
        rowsb0, at = carve(half[1], at, 2, GT * P // 2)
        rowsb0 = rowsb0.bitcast(BF16)
        st0, at = carve(half[1], at, NT, 6)

        at = 0
        xm, at = carve(half[0], at, NT, D)
        w3s, at = carve(half[0], at, E, HC * D)
        XN1, at = carve(half[0], at, 2, GT * D)
        xT1, at = carve(half[0], at, 2, GT * D)
        gw, at = carve(half[0], at, E)
        gb, at = carve(half[0], at, E)
        st1, at = carve(half[0], at, NT, 6)
        tri, at = carve(half[0], at, P // 2)
        tri = tri.bitcast(BF16)
        allone, at = carve(half[0], at, P // 2)
        allone = allone.bitcast(BF16)
        rank_e, at = carve(half[0], at, E)
        iota_t, at = carve(half[0], at, ST)
        iota_r, at = carve(half[0], at, P)
        pair_no, at = carve(half[0], at, PAIRS)
        dump, at = carve(half[0], at, ST)
        assert at <= TPB * N // 2
        at = 0
        w12, at = carve(half[1], at, E, 2 * HID)
        route = at
        TE = NT * E
        oh1, at = carve(half[1], at, TE)
        oh2, at = carve(half[1], at, TE)
        cnt, at = carve(half[1], at, TE)
        run, at = carve(half[1], at, TE)
        pos, at = carve(half[1], at, TE)
        tmp, at = carve(half[1], at, TE)
        ohb, at = carve(half[1], at, TE // 2)
        ohb = ohb.bitcast(BF16)
        seg, at = carve(half[1], at, TE)
        assert at <= TPB * N // 2
        cmpt = half[1][:, route:route + ST * E]
        oh_r, at = carve(half[1], route + ST * E, 2, JC * P)
        oh_t, at = carve(half[1], at, 2, JC * ST)
        assert at <= TPB * N // 2
        gat, at = carve(half[1], route, 2 * 2 * GR, D)
        assert at <= TPB * N // 2
        jf = s2row[:, :].bitcast(F32)
        at = 0
        l12, at = carve(jf, at, 2, NT)
        first_e, at = carve(jf, at, 2, NT)
        wts, at = carve(jf, at, 2, NT)
        slot, at = carve(jf, at, 2, NT)
        slot_ti, at = carve(jf, at, PAIRS)
        slot_ti = slot_ti.bitcast(I32)
        slot_t, at = carve(jf, at, PAIRS)
        slot_r, at = carve(jf, at, PAIRS)
        row, at = carve(jf, at, ST)
        wrap, at = carve(jf, at, ST)
        from_row, at = carve(jf, at, ST)
        from_row = from_row.bitcast(U32)
        to_row, at = carve(jf, at, ST)
        to_row = to_row.bitcast(U32)
        ec, at = carve(jf, at, E)
        et, at = carve(jf, at, E)
        eti, at = carve(jf, at, E)
        eti = eti.bitcast(I32)
        ecum, at = carve(jf, at, E)
        ebase, at = carve(jf, at, E)
        eone, at = carve(jf, at, E)
        tex, at = carve(jf, at, ST)
        texi, at = carve(jf, at, ST)
        texi = texi.bitcast(I32)
        xs, at = carve(jf, at, SU, D)
        lg, at = carve(jf, at, TE)
        assert at <= N // 2
        stf = stage[:, :, :].rearrange("p a b -> p (a b)").bitcast(F32)
        xsT, at = carve(stf, 0, 2, D)
        hidT, at = carve(stf, at, 2, HID)
        ys, at = carve(stf, at, SU, D)
        prf = probs[:, :, :].rearrange("p a b -> p (a b)")
        silu, at = carve(prf, 0, 2, HID)
        hid, at = carve(prf, at, 2, HID)
        lnt, at = carve(prf, at, 7, NT)

        w_in = sem("w_in")
        x_in = [sem(f"x_in{c}") for c in range(4)]
        const_done = sem("const_done")
        pre = sem("pre")
        pe_pre = sem("pe_pre")
        stats_done = sem("stats_done")
        var_ready = sem("var_ready")
        sd_ready = sem("sd_ready")
        ln_chain = sem("ln_chain")
        xn_ready = sem("xn_ready")
        xn_kept = sem("xn_kept")
        xt_done = sem("xt_done")
        xt_ready = sem("xt_ready")
        lin_done = sem("lin_done")
        lin_read = sem("lin_read")
        rows_ready = sem("rows_ready")
        rows_out = [sem("rows_out0"), sem("rows_out1")]
        s2_in = sem("s2_in")
        mean_ready = sem("mean_ready")
        mean_read = sem("mean_read")
        adj_in = [sem("adj_in0"), sem("adj_in1")]
        s1_in = [sem("s1_in0"), sem("s1_in1")]
        nonedge_done = sem("nonedge_done")
        piece_done = sem("piece_done")
        vmax = sem("vmax")
        mval_ready = sem("mval_ready")
        mask_ready = sem("mask_ready")
        act_masks = sem("act_masks")
        trans_done = sem("trans_done")
        logit_ready = sem("logit_ready")
        probs_ready = sem("probs_ready")
        prod_done = sem("prod_done")
        num_ready = sem("num_ready")
        proj_done = sem("proj_done")
        xres_in = sem("xres_in")
        fin = sem("fin")
        xmid_ready = sem("xmid_ready")
        xmid_out = sem("xmid_out")
        we_in = sem("we_in")
        w12_in = sem("w12_in")
        xm_in = sem("xm_in")
        xm_last = sem("xm_last")
        gconst = sem("gconst")
        rt = sem("rt")
        oh_ready = sem("oh_ready")
        cnt_done = sem("cnt_done")
        ed_ready = sem("ed_ready")
        ee_ready = sem("ee_ready")
        tex_ready = sem("tex_ready")
        hots_ready = sem("hots_ready")
        pairs_done = sem("pairs_done")
        rows_known = sem("rows_known")
        x2_out = sem("x2_out")
        xs_in = [sem(f"xs_in{i}") for i in range(SU)]
        xsT_done = sem("xsT_done")
        xsT_ready = sem("xsT_ready")
        h_done = sem("h_done")
        silu_ready = sem("silu_ready")
        hid_ready = sem("hid_ready")
        hT_done = sem("hT_done")
        hT_ready = sem("hT_ready")
        y_done = sem("y_done")
        y_ready = sem("y_ready")
        y_out = [sem(f"y_out{i}") for i in range(SU)]
        res_in = [sem("res_in0"), sem("res_in1")]
        comb1 = sem("comb1")
        comb2 = sem("comb2")
        out_done = sem("out_done")

        maskT = [bank[0], bank[1]]
        logit = [bank[2], bank[3]]
        acc = [bank[4], bank[5]]
        proj = [bank[6], bank[7]]
        tp_bf = [b[:, :].bitcast(BF16)[:, 0:BLK] for b in maskT]

        x_t = x.rearrange("(t p) d -> p t d", p=P)
        xmid_t = xmid_d.rearrange("(t p) d -> p t d", p=P)
        out_t = out.rearrange("(t p) d -> p t d", p=P)

        block = ctx.enter_context(nc.Block())

        @block.sync
        def _(sp):
            sp.dma_start(Wn, W).then_inc(w_in, 16)
            sp.dma_start(acol, a_vec.rearrange("(k o) -> o k", o=D), allow_slow_non_contiguous=True).then_inc(w_in, 16)
            sp.dma_start(bcol, b_W.rearrange("(o a) -> o a", a=1)).then_inc(w_in, 16)
            for c in range(4):
                n = NT // 4
                sp.dma_start(X[:, c * n:(c + 1) * n, :], x_t[:, c * n:(c + 1) * n, :]).then_inc(x_in[c], 16)
            sp.wait_ge(const_done, 1)
            sp.dma_start(ba[P - 1:P, :], b_a.rearrange("(o a) -> o a", a=1)).then_inc(w_in, 16)

            def load_chunk(b, m):
                k, c = m // CPT, m % CPT
                if not (isinstance(b, int) and b == 0 and m < 2):
                    sp.wait_ge(nonedge_done, (b * CPB + m - 1) * PPC)
                sp.dma_start(stage[:, m % 2, :], adj[bass.ds((b * TPB + k) * P, P), c * CH:(c + 1) * CH]
                             ).then_inc(adj_in[m % 2], 16)

            def load_chunks(b, more):
                for m in range(2, CPB):
                    load_chunk(b, m)
                if more:
                    for m in range(2):
                        load_chunk(b + 1, m)

            def load_s1(b, q):
                sp.dma_start(s1row[:, q, :], s1_d[0:1, bass.ds(b * BLK, BLK)].partition_broadcast(P)
                             ).then_inc(s1_in[q], 16)

            def store_xmid(b):
                sp.wait_ge(xmid_ready, b + 1)
                sp.dma_start(xmid_t[:, bass.ds(b * TPB, TPB), :], xres[:, :, :]).then_inc(xmid_out, 16)

            def first_chunk(c, k):
                sp.dma_start(stage[:, k % 2, :], adj[k * P:(k + 1) * P, bass.ds(c * CH, CH)]
                             ).then_inc(adj_in[k % 2], 16)

            def column(c, last=False):
                for k in range(TPB):
                    g, u = TPB * c + k, k % 2
                    sp.wait_ge(nonedge_done, (g + 1) * PPC)
                    if k < 2:
                        first_chunk(c, k + 2)
                    elif not last:
                        first_chunk(c + 1, k - 2)
                    else:
                        sp.dma_start(stage[:, u, :], adj[BLK:BLK + P, u * CH:(u + 1) * CH]).then_inc(adj_in[u], 16)
                    sp.wait_ge(rows_ready, g + 1)
                    sp.dma_start(s1_d[0:1, bass.ds(g * GT * P, GT * P)], rows0[0:1, u, :]).then_inc(rows_out[u], 16)
                    sp.dma_start(s2_d[0:1, bass.ds(g * GT * P, GT * P)], rowsb0[1:2, u, :]).then_inc(rows_out[u], 16)
                for u in range(2):
                    sp.wait_ge(rows_out[u], 32 * (TPB // 2) * (c + 1))
                cols = bass.ds(c * CH, CH)
                sp.dma_start(s2row[:, cols], s2_d[0:1, cols].partition_broadcast(P)).then_inc(s2_in, 16)

            assert GT * P * TPB == CH
            for m in range(2):
                first_chunk(0, m)
            with sp.Fori(0, CPT - 1) as c:
                column(c)
            column(CPT - 1, last=True)
            for q in range(2):
                load_s1(q, q)

            def next_s1(b, q):
                sp.wait_ge(logit_ready, NT * (b + 1))
                load_s1(b + 2, q)

            load_chunks(1, True)
            next_s1(0, 0)
            with sp.Fori(0, (NB - 4) // 2) as i:
                for q in range(2):
                    b = 2 * i + 1 + q
                    load_chunks(b + 1, True)
                    store_xmid(b - 1)
                    next_s1(b, 1 - q)
            load_chunks(NB - 2, True)
            store_xmid(NB - 4)
            next_s1(NB - 3, 1)
            load_chunks(NB - 1, False)
            store_xmid(NB - 3)
            def load_xm(c, n, signal):
                sp.dma_start(xm[:, c * n:(c + 1) * n, :], xmid_t[:, c * n:(c + 1) * n, :]).then_inc(signal, 16)

            sp.wait_ge(trans_done, NT * (NB - 1))
            sp.wait_ge(xmid_out, 16 * (NB - NB // 4))
            for c in range(3):
                load_xm(c, NT // 4, xm_in)
            for c in range(HC):
                sp.dma_start(w3s[:, :, c * D:(c + 1) * D],
                             w3[:, c * P:(c + 1) * P, :].rearrange("e h o -> h e o")).then_inc(we_in, 16)
            sp.dma_start(gw, gate_w).then_inc(we_in, 16)
            sp.dma_start(gb, gate_b.rearrange("(a e) -> a e", a=1).partition_broadcast(P)).then_inc(we_in, 16)
            store_xmid(NB - 2)
            store_xmid(NB - 1)
            sp.wait_ge(xmid_out, 16 * NB)
            load_xm(3, NT // 4, xm_last)
            sp.wait_ge(trans_done, NT * NB)
            w12v = w12.rearrange("p e (k h) -> p e k h", k=2)
            sp.dma_start(w12v[:, :, 0, :], w1.rearrange("e d h -> d e h")).then_inc(w12_in, 16)
            sp.dma_start(w12v[:, :, 1, :], w2.rearrange("e d h -> d e h")).then_inc(w12_in, 16)

            x2_t = x2_d.rearrange("(t p) d -> p t d", p=P)
            for c in range(4):
                n = NT // 4
                sp.wait_ge(xn_kept, NG + NG // 4 * (c + 1))
                sp.dma_start(x2_t[:, c * n:(c + 1) * n, :], X[:, c * n:(c + 1) * n, :]).then_inc(x2_out, 16)

            for u in range(SU):
                sp.wait_ge(y_out[u], 16 * (ST // SU))
            res_t = res_d[0:2 * N, :].rearrange("(c t p) d -> c p t d", c=2, p=P)

            def load_results(n, u, first):
                if not first:
                    sp.wait_ge(comb2, GR * (n - 1))
                for c in range(2):
                    sp.dma_start(gat[:, (2 * u + c) * GR:(2 * u + c + 1) * GR, :], res_t[c, :, bass.ds(GR * n, GR), :]
                                 ).then_inc(res_in[u], 16)

            def store_out(n):
                sp.wait_ge(comb2, GR * n + GR)
                sp.dma_start(out_t[:, bass.ds(GR * n, GR), :], xm[:, bass.ds(GR * n, GR), :]).then_inc(out_done, 16)

            for n in range(2):
                load_results(n, n, True)
            with sp.Fori(0, NT // GR // 2 - 1) as i:
                for u in range(2):
                    load_results(2 * i + u + 2, u, False)
                    store_out(2 * i + u)
            for u in range(2):
                store_out(NT // GR - 2 + u)
            sp.wait_ge(out_done, 16 * (NT // GR))

        @block.gpsimd
        def _(pool):
            pool.memset(pcarrier[:, :], 0.0)
            pool.memset(ba, 0.0).then_inc(const_done, 1)
            pool.memset(ident[:, :], 0.0).then_inc(const_done, 1)
            pool.memset(identf[:, :], 0.0).then_inc(const_done, 1)
            pool.wait_ge(const_done, 3)
            for m in (ident, identf):
                pool.affine_select(out=m[:, :], in_=m[:, :], compare_op=ALU.not_equal, fill=1.0, base=0,
                                   pattern=[[-1, P]], channel_multiplier=1).then_inc(const_done, 1)
            pool.memset(Wx[:, D:D + 1], 0.0).then_inc(const_done, 1)
            pool.wait_ge(const_done, 6)
            pool.affine_select(out=Wx[:, D:D + 1], in_=Wx[:, D:D + 1], compare_op=ALU.not_equal, fill=1.0,
                               base=-(P - 1), pattern=[[0, 1]], channel_multiplier=1).then_inc(const_done, 1)
            for u in range(2):
                pool.memset(XN0[:, u, :].rearrange("p (k d) -> p k d", d=D)[:, :, D - 1:D], 1.0
                            ).then_inc(const_done, 1)

            def make_masks(b, q, tiles=TPB):
                for k in range(tiles):
                    if not (isinstance(b, int) and b == k == 0):
                        pool.wait_ge(mask_ready, b * CPB + k * CPT)
                    pool.wait_ge(mval_ready, b * TPB + k + 1)
                    pool.tensor_tensor(pcarrier[:, 1:2], pcarrier[:, 0:1], pcarrier[:, 0:1], ALU.add)
                    for c in range(CPT):
                        m = maskn[q][k][:, c * CH:(c + 1) * CH]
                        pool.tensor_scalar(m, m, -1.0, mval[:, q, k:k + 1], ALU.mult, ALU.add
                                           ).then_inc(mask_ready, 1)

            def load_xres(b, first=False):
                if not first:
                    pool.wait_ge(xmid_out, 16 * b)
                pool.dma_start(xres[:, :, :], x_t[:, bass.ds(b * TPB, TPB), :]).then_inc(xres_in, 16)

            make_masks(0, 0, TPB // 2)
            pool.wait_ge(mask_ready, CPB // 2)
            pool.wait_ge(act_masks, TPB // 2)
            pool.tensor_tensor(pcarrier[:, 1:2], pcarrier[:, 0:1], pcarrier[:, 0:1], ALU.add
                               ).then_inc(mask_ready, CPB // 2)
            load_xres(0, True)
            make_masks(1, 1)
            with pool.Fori(0, (NB - 2) // 2) as i:
                for q in range(2):
                    b = 2 * i + 1 + q
                    make_masks(b + 1, q)
                    load_xres(b)
            load_xres(NB - 1)

            pool.wait_ge(trans_done, NT * (NB - 1))
            pool.memset(tri, 1.0).then_inc(gconst, 1)
            pool.memset(allone, 1.0).then_inc(gconst, 1)
            pool.iota(rank_e, pattern=[[-1, E]], base=E, channel_multiplier=0,
                      allow_small_or_imprecise_dtypes=True).then_inc(gconst, 1)
            pool.iota(iota_t, pattern=[[1, ST]], base=0, channel_multiplier=0,
                      allow_small_or_imprecise_dtypes=True).then_inc(gconst, 1)
            pool.iota(iota_r, pattern=[[1, P]], base=0, channel_multiplier=0,
                      allow_small_or_imprecise_dtypes=True).then_inc(gconst, 1)
            pool.iota(pair_no, pattern=[[P, PAIRS]], base=1, channel_multiplier=1,
                      allow_small_or_imprecise_dtypes=True).then_inc(gconst, 1)
            pool.iota(dump, pattern=[[P, ST]], base=2 * N + 1, channel_multiplier=1,
                      allow_small_or_imprecise_dtypes=True).then_inc(gconst, 1)
            pool.wait_ge(gconst, 1)
            pool.affine_select(out=tri, in_=tri, compare_op=ALU.is_gt, fill=0.0, base=0,
                               pattern=[[1, P]], channel_multiplier=-1).then_inc(gconst, 1)
            pool.wait_ge(mval_ready, NT)
            pool.memset(eone, 1.0).then_inc(gconst, 1)

            pool.wait_ge(x2_out, 64)
            pool.wait_ge(rows_known, 2)
            BEHIND = 5
            for i in range(ST + BEHIND):
                if i < ST:
                    if i >= SU:
                        pool.wait_ge(xsT_done, i - SU + 1)
                    pool.indirect_dma_start(
                        out=xs[:, i % SU, :], out_offset=None, in_=x2_d[:, :],
                        in_offset=bass.IndirectOffsetOnAxis(ap=from_row[:, i:i + 1], axis=0)
                    ).then_inc(xs_in[i % SU], 16)
                k = i - BEHIND
                if k >= 0:
                    pool.wait_ge(y_ready, k + 1)
                    pool.indirect_dma_start(
                        out=res_d[:, :], out_offset=bass.IndirectOffsetOnAxis(ap=to_row[:, k:k + 1], axis=0),
                        in_=ys[:, k % SU, :], in_offset=None).then_inc(y_out[k % SU], 16)

        @block.scalar
        def _(act):
            def roots(s):
                act.wait_ge(var_ready, s + 1)
                act.activation(lnt[:, 1, :], lnt[:, 0, :], ACT.Sqrt).then_inc(sd_ready, 1)

            def ln_group(g, u, s, XN, xT, first=False):
                n = NG * s + g
                act.wait_ge(xn_ready, n + 1)
                act.activation(X[:, bass.ds(GT * g, GT), :], XN[:, u, :].rearrange("p (k d) -> p k d", d=D),
                               ACT.Copy).then_inc(xn_kept, 1)
                act.wait_ge(xt_done, n + 1)
                if not first:
                    act.wait_ge(lin_done, n - 1)
                act.activation(xT[:, u, :], maskT[u][:, :], ACT.Copy).then_inc(xt_ready, 1)

            def first_nonedge(g, u, i):
                act.wait_ge(adj_in[u], 8 * (g - u) + 16)
                act.activation(big[:, bass.ds((i % 2 * 2 + u) * N + i // 2 * CH, CH)], stage[:, u, :], ACT.Relu,
                               bias=bigc[:, 0:1], scale=-BIG).then_inc(nonedge_done, PPC)

            act.wait_ge(pre, 1)
            roots(0)
            for g in range(2):
                ln_group(g, g, 0, XN0, xT0, True)
                first_nonedge(g, g, 0)
            with act.Fori(1, NG // 2) as i:
                for u in range(2):
                    ln_group(2 * i + u, u, 0, XN0, xT0)
                    first_nonedge(2 * i + u, u, i)

            for k in range(TPB // 2, TPB):
                act.wait_ge(mval_ready, k + 1)
                act.activation(maskn[0][k], maskn[0][k], ACT.Identity, bias=mval[:, 0, k:k + 1], scale=-1.0
                               ).then_inc(act_masks, 1)

            def nonedge(b, q, m, h):
                k, c = m // CPT, m % CPT
                if m == h == 0 and not (isinstance(b, int) and b < 2):
                    act.wait_ge(trans_done, NT * (b - 1))
                if h == 0:
                    act.wait_ge(adj_in[m % 2], 8 * (b * CPB + m - m % 2) + 16)
                lo = c * CH + h * PC
                act.activation(maskn[q][k][:, lo:lo + PC], stage[:, m % 2, h * PC:(h + 1) * PC], ACT.Relu,
                               bias=bigc[:, 0:1], scale=-BIG).then_inc(nonedge_done, 1)

            def exps(b, j, q, first=False):
                n = NT * b + j
                act.wait_ge(logit_ready, n + 1)
                if not (first and j < PR):
                    act.wait_ge(prod_done, n - PR + 1)
                act.activation(probs[:, j % PR, :], logit[j % 2][:, :], ACT.Exp, bias=scol[:, j, 1:2],
                               scale=RISE).then_inc(probs_ready, 1)

            def numerators(b, q, first=False):
                act.wait_ge(prod_done, NT * (b + 1))
                if not first:
                    act.wait_ge(proj_done, b)
                act.activation(numT[:, :], acc[q][:, :], ACT.Copy).then_inc(num_ready, 1)

            def run_block(b, q, first=False, last=False, second=False):
                for j in range(NT):
                    exps(b, j, q, first)
                    if not last and j in NONEDGE_AT:
                        i = NONEDGE_AT[j]
                        nonedge(b + 1, 1 - q, i // PPC, i % PPC)
                    if j == 4 and not first:
                        numerators(b - 1, 1 - q, second)

            run_block(0, 0, first=True)
            run_block(1, 1, second=True)
            with act.Fori(1, NB // 2 - 1) as i:
                for q in range(2):
                    run_block(2 * i + q, q)
            run_block(NB - 2, 0)
            run_block(NB - 1, 1, last=True)
            numerators(NB - 1, 1)

            roots(1)
            with act.Fori(0, NG // 2) as i:
                for u in range(2):
                    ln_group(2 * i + u, u, 1, XN1, xT1)
            act.wait_ge(ed_ready, 1)
            act.activation(wts[:, 1, :], l12[:, 0, :], ACT.Exp).then_inc(ee_ready, 1)

            def copy_xsT(i, v, first):
                act.wait_ge(xsT_done, i + 1)
                if not first:
                    act.wait_ge(h_done, i - 1)
                act.activation(xsT[:, v, :], bank[v][:, 0:P], ACT.Copy).then_inc(xsT_ready, 1)

            def do_silu(i, v, first):
                act.wait_ge(h_done, i + 1)
                if not first:
                    act.wait_ge(hid_ready, i - 1)
                act.activation(silu[:, v, :], bank[2 + v][:, 0:HID], ACT.Silu).then_inc(silu_ready, 1)

            def copy_y(i, u, first):
                act.wait_ge(y_done, i + 1)
                if not first:
                    act.wait_ge(y_out[u], 16 * (i // SU))
                act.activation(ys[:, u, :], bank[6 + u % 2][:, 0:D], ACT.Copy).then_inc(y_ready, 1)

            def step(i, u, lo, hi, first):
                if hi >= 1:
                    copy_xsT(i + 1, (u + 1) % 2, first and i + 1 < 2)
                if hi >= 0:
                    do_silu(i, u % 2, first and i < 2)
                if lo >= 2:
                    copy_y(i - 2, (u - 2) % SU, first and i - 2 < SU)

            copy_xsT(0, 0, True)
            for i in range(2 * SU):
                step(i, i % SU, i, 9, i < SU + 2)
            with act.Fori(2, ST // SU - 1) as g:
                for u in range(SU):
                    i = SU * g + u
                    copy_xsT(i + 1, (u + 1) % 2, False)
                    do_silu(i, u % 2, False)
                    act.wait_ge(y_done, i - 1)
                    act.wait_ge(y_out[(u - 2) % SU], 16 * (g if u >= 2 else g - 1))
                    act.activation(ys[:, (u - 2) % SU, :], bank[6 + u % 2][:, 0:D], ACT.Copy).then_inc(y_ready, 1)
            for i in range(ST - SU, ST + 2):
                step(i, i % SU, 9, ST - 1 - i, False)

        @block.tensor
        def _(pe):
            pe.wait_ge(const_done, 5)
            pe.wait_ge(pre, 2)
            pe.transpose(bank[0][:, 0:P], Wn, identf[:, :]).then_inc(pe_pre, 1)
            pe.matmul(bank[1][:, 0:2], Wn, acol, start=True, stop=True).then_inc(pe_pre, 1)
            pe.wait_ge(pre, 4)

            def transpose_group(g, u, s, XN, read):
                n = NG * s + g
                pe.wait_ge(xn_ready, n + 1)
                if read:
                    pe.wait_ge(xt_ready, n - 1)
                for k in range(GT):
                    t = pe.transpose(maskT[u][:, k * P:(k + 1) * P], XN[:, u, k * D:(k + 1) * D], identf[:, :])
                t.then_inc(xt_done, 1)

            def group0(g, u, read):
                pe.wait_ge(xt_ready, g + 1)
                if read:
                    pe.wait_ge(lin_read, g - 1)
                pe.matmul(logit[u][0:2, :], V, xT0[:, u, :], start=True, stop=True)
                for k in range(GT):
                    m = pe.matmul(acc[u][:, 2 * k:2 * k + 2], xT0[:, u, k * P:(k + 1) * P], V, start=True, stop=True)
                m.then_inc(lin_done, 1)

            transpose_group(0, 0, 0, XN0, False)
            for g in range(2):
                transpose_group(g + 1, 1 - g, 0, XN0, g > 0)
                group0(g, g, False)
            with pe.Fori(1, NG // 2 - 1) as i:
                for u in range(2):
                    transpose_group(2 * i + u + 1, 1 - u, 0, XN0, True)
                    group0(2 * i + u, u, True)
            transpose_group(NG - 1, 1, 0, XN0, True)
            for u in range(2):
                group0(NG - 2 + u, u, True)
            pe.wait_ge(mean_ready, 1)
            pe.matmul(proj[1][:, 0:1], xsum, onescol[:, 0:1], start=True, stop=True).then_inc(pe_pre, 1)
            pe.wait_ge(mean_ready, 2)
            pe.matmul(proj[0][:, 0:D + 1], xsrep, Wx[:, :], start=True, stop=True).then_inc(pe_pre, 1)

            def transposes(b, j, q, first=False):
                n = NT * b + j
                if j * P % CH == 0:
                    pe.wait_ge(mask_ready, CPB * b + CPB - CPT + j * P // CH + 1)
                if not (first and j < 2):
                    pe.wait_ge(logit_ready, n - 1)
                for k in range(TPB):
                    t = pe.transpose(tp_bf[j % 2][:, k * P:(k + 1) * P], maskn[q][k][:, j * P:(j + 1) * P],
                                     ident[:, :])
                t.then_inc(trans_done, 1)

            def product(b, j, q, first=False):
                n = NT * b + j
                pe.wait_ge(probs_ready, n + 1)
                if j == 0 and not first:
                    pe.wait_ge(num_ready, b - 1)
                pe.matmul(acc[q][:, :], X[:, j, :], probs[:, j % PR, :], start=(j == 0), stop=(j == NT - 1)
                          ).then_inc(prod_done, 1)

            def project(b, first=False):
                pe.wait_ge(num_ready, b + 1)
                if first:
                    pe.wait_ge(mean_read, 1)
                else:
                    pe.wait_ge(xmid_ready, b)
                for k in range(TPB):
                    m = pe.matmul(proj[k // 2][:, k % 2 * (D + 1):(k % 2 + 1) * (D + 1)],
                                  numT[:, k * P:(k + 1) * P], Wx[:, :], start=True, stop=True)
                m.then_inc(proj_done, 1)

            def run_block(b, q, first=False, last=False, second=False):
                for j in range(NT):
                    if j + AHEAD < NT:
                        transposes(b, j + AHEAD, q, first)
                    elif not last:
                        transposes(b + 1, j + AHEAD - NT, 1 - q)
                    product(b, j, q, first or second)
                    if j == 8 and not first:
                        project(b - 1, second)

            pe.wait_ge(xt_ready, NG)
            pe.wait_ge(lin_read, NG)
            for j in range(AHEAD):
                transposes(0, j, 0, first=True)
            run_block(0, 0, first=True)
            run_block(1, 1, second=True)
            with pe.Fori(1, NB // 2 - 1) as i:
                for q in range(2):
                    run_block(2 * i + q, q)
            run_block(NB - 2, 0)
            run_block(NB - 1, 1, last=True)
            project(NB - 1)

            pe.wait_ge(we_in, 16 * (2 + HC))
            pe.wait_ge(gconst, 9)
            pe.wait_ge(logit_ready, NT * NB)
            pe.wait_ge(num_ready, NB)

            def group1(g, u):
                pe.wait_ge(xt_ready, NG + g + 1)
                pe.wait_ge(lin_read, NG + g - 1)
                for k in range(GT):
                    m = pe.matmul(acc[u][:, k * E:(k + 1) * E], xT1[:, u, k * P:(k + 1) * P], gw,
                                  start=True, stop=True)
                m.then_inc(lin_done, 1)

            transpose_group(0, 0, 1, XN1, True)
            with pe.Fori(0, NG // 2 - 1) as i:
                for u in range(2):
                    transpose_group(2 * i + u + 1, 1 - u, 1, XN1, True)
                    group1(2 * i + u, u)
            transpose_group(NG - 1, 1, 1, XN1, True)
            for u in range(2):
                group1(NG - 2 + u, u)

            pe.wait_ge(oh_ready, 1)
            for h in range(2):
                pe.matmul(bank[h][:, :], tri, ohb[:, h * 512:(h + 1) * 512], start=True, stop=True)
            for h in range(2):
                m = pe.matmul(bank[2 + h][:, :], allone, ohb[:, h * 512:(h + 1) * 512], start=True, stop=True)
            m.then_inc(cnt_done, 1)

            def add_pairs(n, u, lo, hi):
                pe.wait_ge(hots_ready, n + 1)
                for j in range(JC):
                    m = pe.matmul(bank[4][:, 0:ST], oh_r[:, u, j * P:(j + 1) * P], oh_t[:, u, j * ST:(j + 1) * ST],
                                  start=(lo and j == 0), stop=(hi and j == JC - 1))
                m.then_inc(pairs_done, 1)

            add_pairs(0, 0, True, False)
            add_pairs(1, 1, False, False)
            with pe.Fori(1, PAIRS // JC // 2 - 1) as i:
                for u in range(2):
                    add_pairs(2 * i + u, u, False, False)
            add_pairs(PAIRS // JC - 2, 0, False, False)
            add_pairs(PAIRS // JC - 1, 1, False, True)
            pe.wait_ge(tex_ready, 1)

            def experts_of(i, n):
                return nc.values_load_multi_w_load_instructions(
                    texi[0:1, bass.ds(i, n)], engines=(mybir.EngineType.PE,), min_val=0, max_val=E - 1,
                    skip_runtime_bounds_check_because="the table's entries are counts of experts, cut at E - 1")[1]

            def t_x(i, u, uses):
                pe.wait_ge(xs_in[u], 16 * uses)
                pe.transpose(bank[u % 2][:, 0:P], xs[:, u, :], identf[:, :]).then_inc(xsT_done, 1)

            def m_h(i, u, e):
                pe.wait_ge(xsT_ready, i + 1)
                pe.matmul(bank[2 + u % 2][:, :], xsT[:, u % 2, :],
                          w12[:, bass.ds(e, 1), :].rearrange("p a b -> p (a b)"), start=True, stop=True
                          ).then_inc(h_done, 1)

            def t_h(i, u):
                pe.wait_ge(hid_ready, i + 1)
                for c in range(HC):
                    t = pe.transpose(bank[4 + u % 2][:, c * P:(c + 1) * P], hid[:, u % 2, c * P:(c + 1) * P],
                                     identf[:, :])
                t.then_inc(hT_done, 1)

            def m_y(i, u, e, first):
                pe.wait_ge(hT_ready, i + 1)
                if not first:
                    pe.wait_ge(y_ready, i - 1)
                for c in range(HC):
                    m = pe.matmul(bank[6 + u % 2][:, 0:D], hidT[:, u % 2, c * P:(c + 1) * P],
                                  w3s[:, bass.ds(e, 1), c * D:(c + 1) * D].rearrange("p a b -> p (a b)"),
                                  start=(c == 0), stop=(c == HC - 1))
                m.then_inc(y_done, 1)

            pe.wait_ge(w12_in, 32)
            e = experts_of(0, SU)
            t_x(0, 0, 1)
            for i in range(SU):
                m_h(i, i, e[i])
                t_x(i + 1, (i + 1) % SU, (i + 1) // SU + 1)
                if i >= 1:
                    t_h(i - 1, i - 1)
                if i >= 2:
                    m_y(i - 2, i - 2, e[i - 2], i - 2 < 2)
            with pe.Fori(1, ST // SU - 1) as g:
                e = experts_of(SU * g - 2, 2) + experts_of(SU * g, SU)
                for u in range(SU):
                    i = SU * g + u
                    m_h(i, u, e[u + 2])
                    t_x(i + 1, (u + 1) % SU, g + 1 if u + 1 < SU else g + 2)
                    t_h(i - 1, (u - 1) % SU)
                    m_y(i - 2, (u - 2) % SU, e[u], False)
            e = experts_of(ST - SU - 2, SU + 2)
            for i in range(ST - SU, ST + 2):
                if i < ST:
                    m_h(i, i % SU, e[i - (ST - SU - 2)])
                if i + 1 < ST:
                    t_x(i + 1, (i + 1) % SU, (i + 1) // SU + 1)
                if i - 1 < ST:
                    t_h(i - 1, (i - 1) % SU)
                m_y(i - 2, (i - 2) % SU, e[i - (ST - SU)], False)

        @block.vector
        def _(dve):
            dve.memset(bigc[:, :], BIG).then_inc(pre, 1)
            dve.memset(onescol[:, :], 1.0)
            dve.wait_ge(w_in, 64)
            dve.tensor_copy(wlast[:, :], Wn[:, D - 1:D]).then_inc(ln_chain, 1)
            dve.wait_ge(ln_chain, 1)
            dve.tensor_scalar(Wn[:, 0:D - 1], Wn[:, 0:D - 1], wlast[:, 0:1], None, ALU.subtract)
            dve.tensor_copy(Wn[:, D - 1:D], bcol).then_inc(pre, 1)
            dve.wait_ge(pe_pre, 2)
            dve.tensor_copy(Wx[:, 0:D], bank[0][:, 0:P]).then_inc(pre, 1)
            dve.tensor_copy(V[:, 1:2], bank[1][:, 1:2])
            dve.tensor_tensor(V[:, 0:1], bank[1][:, 0:1], ba, ALU.add).then_inc(pre, 1)
            PRE = 1

            links = [PRE]

            def link(ins):
                links[0] += 1
                ins.then_inc(ln_chain, 1)
                dve.wait_ge(ln_chain, links[0])

            def ln_stats(s, src, st, loads):
                for lo, hi, loaded, count in loads:
                    dve.wait_ge(loaded, count)
                    with dve.Fori(lo, hi) as g:
                        for k in range(GT):
                            ins = dve.bn_stats(st[:, bass.ds(GT * g + k, 1), :].rearrange("p a d -> p (a d)"),
                                               src[:, bass.ds(GT * g + k, 1), :].rearrange("p a d -> p (a d)"))
                        ins.then_inc(stats_done, 1)
                dve.wait_ge(stats_done, NG * (s + 1))
                link(dve.tensor_tensor(lnt[:, 2, :], st[:, :, 1], st[:, :, 4], ALU.subtract))
                link(dve.tensor_tensor(lnt[:, 3, :], lnt[:, 2, :], lnt[:, 2, :], ALU.mult))
                link(dve.tensor_tensor(lnt[:, 4, :], st[:, :, 2], st[:, :, 5], ALU.add))
                link(dve.tensor_scalar(lnt[:, 2, :], lnt[:, 4, :], 1.0 / D, EPS, ALU.mult, ALU.add))
                dve.scalar_tensor_tensor(out=lnt[:, 0, :], in0=lnt[:, 3, :], scalar=0.25, in1=lnt[:, 2, :],
                                         op0=ALU.mult, op1=ALU.add).then_inc(var_ready, 1)
                link(dve.tensor_tensor(lnt[:, 4, :], st[:, :, 1], st[:, :, 4], ALU.add))
                link(dve.tensor_scalar(lnt[:, 6, :], lnt[:, 4, :], 0.5, None, ALU.mult))
                dve.wait_ge(sd_ready, s + 1)
                link(dve.reciprocal(lnt[:, 2, :], lnt[:, 1, :]))
                link(dve.tensor_tensor(lnt[:, 3, :], lnt[:, 2, :], lnt[:, 2, :], ALU.mult))
                link(dve.tensor_tensor(lnt[:, 4, :], lnt[:, 3, :], lnt[:, 0, :], ALU.mult))
                link(dve.tensor_scalar(lnt[:, 3, :], lnt[:, 4, :], -0.5, 1.5, ALU.mult, ALU.add))
                link(dve.tensor_tensor(lnt[:, 5, :], lnt[:, 2, :], lnt[:, 3, :], ALU.mult))

            def normalise(s, g, u, XN, src, ncol, first=False):
                n = NG * s + g
                if not first:
                    dve.wait_ge(xn_kept, n - 1)
                    dve.wait_ge(xt_done, n - 1)
                for k in range(GT):
                    t = bass.ds(GT * g + k, 1)
                    ins = dve.tensor_scalar(XN[:, u, k * D:k * D + ncol],
                                            src[:, t, 0:ncol].rearrange("p a d -> p (a d)"),
                                            lnt[:, 6, t], lnt[:, 5, t], ALU.subtract, ALU.mult)
                ins.then_inc(xn_ready, 1)

            def read_group0(g, u, turn):
                dve.wait_ge(lin_done, g + 1)
                if turn is not None:
                    dve.wait_ge(rows_out[u], 32 * turn)
                dve.tensor_copy(rows0[0:2, u, :], logit[u][0:2, :])
                dve.tensor_copy(rowsb0[0:2, u, :], logit[u][0:2, :]).then_inc(rows_ready, 1)
                dve.tensor_copy(scol[:, bass.ds(GT * g, GT), :],
                                acc[u][:, 0:2 * GT].rearrange("p (k s) -> p k s", s=2)).then_inc(lin_read, 1)

            VLINKS = 1 + 2 * TPB

            def piece(b, q, k, c, h):
                if k == c == h == 0:
                    dve.tensor_copy(s1cur[:, q, :], scol[:, bass.ds(TPB * b, TPB), 0]).then_inc(vmax, 1)
                lo = c * CH + h * PC
                dve.tensor_tensor_reduce(scrap[:, h, :], s2row[:, lo:lo + PC], maskn[q][k][:, lo:lo + PC], 1.0, -3e38,
                                         ALU.subtract, ALU.max,
                                         part[:, k, lo // PC:lo // PC + 1]).then_inc(piece_done, 1)

            def row_end(b, q, k, step, pieces=None):
                before = VLINKS * b + 1 + 2 * k
                if step == 0:
                    dve.wait_ge(piece_done, (b * TPB + k + 1) * PPT if pieces is None else pieces)
                    dve.tensor_reduce(rmax[:, k:k + 1], part[:, k, :], AX.X, ALU.max).then_inc(vmax, 1)
                elif step == 1:
                    dve.wait_ge(vmax, before + 1)
                    dve.tensor_scalar(amax[:, k:k + 1], rmax[:, k:k + 1], -1.0, s1cur[:, q, k:k + 1],
                                      ALU.mult, ALU.max).then_inc(vmax, 1)
                else:
                    dve.wait_ge(vmax, before + 2)
                    if not (isinstance(b, int) and b < 2):
                        dve.wait_ge(mask_ready, CPB * (b - 2) + CPT * (k + 1))
                    dve.scalar_tensor_tensor(out=mval[:, q, k:k + 1], in0=rmax[:, k:k + 1], scalar=-1.0 / RISE,
                                             in1=amax[:, k:k + 1], op0=ALU.mult, op1=ALU.subtract
                                             ).then_inc(mval_ready, 1)

            def first_pieces(n):
                c, k = n // TPB, n % TPB
                dve.wait_ge(s2_in, 16 * (c + 1))
                dve.wait_ge(nonedge_done, (n + 1) * PPC)
                for h in range(PPC):
                    if n:
                        dve.wait_ge(piece_done, PPC * n + h - 1)
                    piece(0, 0, k, c, h)
                if c == CPT - 1:
                    for step in range(3):
                        row_end(0, 0, k, step, PPC * (n + 1))

            dve.wait_ge(const_done, 9)
            ln_stats(0, X, st0, [(NG // 4 * c, NG // 4 * (c + 1), x_in[c], 16) for c in range(4)])
            for g in range(2):
                normalise(0, g, g, XN0, X, D - 1, True)
            for g in range(2):
                normalise(0, g + 2, g, XN0, X, D - 1)
                read_group0(g, g, None)
            with dve.Fori(1, 3) as turn:
                for u in range(2):
                    normalise(0, 2 * turn + u + 2, u, XN0, X, D - 1)
                    read_group0(2 * turn + u, u, turn)
            for g in range(6, NG):
                if g + 2 < NG:
                    normalise(0, g + 2, g % 2, XN0, X, D - 1)
                read_group0(g, g % 2, g // 2)
                first_pieces(g - 6)
            dve.wait_ge(lin_read, NG)
            dve.tensor_scalar(ns2[:, :], scol[:, :, 1], -1.0, None, ALU.mult)
            dve.wait_ge(xn_kept, NG)
            dve.tensor_reduce(xsum, X[:, :, :].rearrange("p t d -> p d t"), AX.X, ALU.add).then_inc(mean_ready, 1)
            dve.wait_ge(pe_pre, 3)
            dve.tensor_copy(xsrep, proj[1][:, 0:1].to_broadcast([P, P])).then_inc(mean_ready, 1)
            dve.wait_ge(pe_pre, 4)
            dve.tensor_copy(mean_row[:, :], proj[0][:, 0:D + 1]).then_inc(mean_read, 1)
            for n in range(NG - 6, CPB):
                first_pieces(n)

            FLINKS = 4

            def logits(b, j, q, i, first):
                n = NT * b + j
                if j == 0:
                    dve.wait_ge(s1_in[q], 16 * (i + 1))
                dve.wait_ge(trans_done, n + 1)
                if not (first and j < 2):
                    dve.wait_ge(probs_ready, n - 1)
                dve.scalar_tensor_tensor(out=logit[j % 2][:, :], in0=s1row[:, q, :], scalar=ns2[:, j:j + 1],
                                         in1=tp_bf[j % 2], op0=ALU.max, op1=ALU.add).then_inc(logit_ready, 1)

            def finish(b, part_of):
                before = FLINKS * b
                def link(ins, n):
                    ins.then_inc(fin, 1)
                    dve.wait_ge(fin, before + n)

                k = (part_of - 2) % TPB
                if part_of == 0:
                    dve.wait_ge(proj_done, b + 1)
                    for h in range(2):
                        ins = dve.tensor_scalar(noedge[:, 2 * h:2 * h + 2], proj[h][:, D:2 * D + 2:D + 1], 0.0, None,
                                                ALU.is_equal)
                    link(ins, 1)
                    for h in range(2):
                        ins = dve.scalar_tensor_tensor(out=den[:, 2 * h:2 * h + 2], in0=noedge[:, 2 * h:2 * h + 2],
                                                       scalar=mean_row[:, D:D + 1],
                                                       in1=proj[h][:, D:2 * D + 2:D + 1], op0=ALU.mult, op1=ALU.add)
                    link(ins, 2)
                elif part_of == 1:
                    link(dve.reciprocal(rden[:, :], den[:, :]), 3)
                    dve.tensor_tensor(nshare[:, :], noedge[:, :], rden[:, :], ALU.mult)
                    dve.wait_ge(xres_in, 16 * (b + 1))
                elif part_of < 2 + TPB:
                    ins = dve.scalar_tensor_tensor(out=xres[:, k, :],
                                                   in0=proj[k // 2][:, k % 2 * (D + 1):k % 2 * (D + 1) + D],
                                                   scalar=rden[:, k:k + 1], in1=xres[:, k, :],
                                                   op0=ALU.mult, op1=ALU.add)
                    if k == TPB - 1:
                        link(ins, 4)
                else:
                    ins = dve.scalar_tensor_tensor(out=xres[:, k, :], in0=mean_row[:, 0:D],
                                                   scalar=nshare[:, k:k + 1], in1=xres[:, k, :],
                                                   op0=ALU.mult, op1=ALU.add)
                    if k == TPB - 1:
                        ins.then_inc(xmid_ready, 1)

            FPARTS = 2 + 2 * TPB

            def run_block(b, q, i, first=False, last=False):
                for j in range(NT):
                    if not last and j in PIECE_AT:
                        m, h = PIECE_AT[j]
                        dve.wait_ge(nonedge_done, (b + 1) * PPB + m * PPC + h + 1)
                    logits(b, j, q, i, first)
                    if not last and j in PIECE_AT:
                        piece(b + 1, 1 - q, m // CPT, m % CPT, h)
                    if not last and j in ROW_END_AT:
                        k, steps = ROW_END_AT[j]
                        for step in steps:
                            row_end(b + 1, 1 - q, k, step)
                    if not first and j in END_AT[:FPARTS]:
                        finish(b - 1, END_AT.index(j))

            run_block(0, 0, 0, first=True)
            run_block(1, 1, 0)
            with dve.Fori(1, NB // 2 - 1) as i:
                for q in range(2):
                    run_block(2 * i + q, q, i)
            run_block(NB - 2, 0, NB // 2 - 1)
            run_block(NB - 1, 1, NB // 2 - 1, last=True)
            for f in range(FPARTS):
                finish(NB - 1, f)

            dve.wait_ge(trans_done, NT * (NB - 1))
            ln_stats(1, xm, st1, ((0, NG - NG // 4, xm_in, 48), (NG - NG // 4, NG, xm_last, 16)))

            def read_group1(g, u):
                dve.wait_ge(lin_done, NG + g + 1)
                dve.tensor_scalar(lg[:, bass.ds(g * GT * E, GT * E)], acc[u][:, 0:GT * E], 0.0, None, ALU.add
                                  ).then_inc(lin_read, 1)

            for g in range(2):
                normalise(1, g, g, XN1, xm, D)
            with dve.Fori(0, NG // 2 - 1) as turn:
                for u in range(2):
                    normalise(1, 2 * turn + u + 2, u, XN1, xm, D)
                    read_group1(2 * turn + u, u)
            for u in range(2):
                read_group1(NG - 2 + u, u)
            dve.wait_ge(lin_read, 2 * NG)

            rts = [0]

            def link(ins):
                rts[0] += 1
                ins.then_inc(rt, 1)
                dve.wait_ge(rt, rts[0])

            def by_te(v):
                return v.rearrange("p (t e) -> p t e", e=E)

            def by_et(v):
                return v.rearrange("p (e t) -> p e t", e=E)

            def per_t(v):
                return v.unsqueeze(2).to_broadcast([P, NT, E])

            dve.wait_ge(gconst, 9)
            dve.wait_ge(we_in, 16 * (2 + HC))
            link(dve.tensor_tensor(by_te(lg), by_te(lg), gb.unsqueeze(1).to_broadcast([P, NT, E]), ALU.add))
            link(dve.memset(seg, 1.0))
            link(dve.memset(by_et(seg)[:, :, 0:1], 0.0))
            rank = rank_e.unsqueeze(1).to_broadcast([P, NT, E])
            for c, oh in enumerate((oh1, oh2)):
                link(dve.tensor_reduce(l12[:, c, :], by_te(lg), AX.X, ALU.max))
                link(dve.tensor_tensor(by_te(tmp), by_te(lg), per_t(l12[:, c, :]), ALU.is_equal))
                link(dve.tensor_tensor(by_te(pos), by_te(tmp), rank, ALU.mult))
                link(dve.tensor_reduce(first_e[:, c, :], by_te(pos), AX.X, ALU.max))
                link(dve.tensor_tensor(by_te(oh), rank, per_t(first_e[:, c, :]), ALU.is_equal))
                if c == 0:
                    link(dve.scalar_tensor_tensor(out=lg, in0=oh, scalar=-3e38, in1=lg, op0=ALU.mult, op1=ALU.add))
            dve.tensor_tensor(ohb, oh1, oh2, ALU.add).then_inc(oh_ready, 1)
            link(dve.tensor_tensor(first_e[:, 0, :], l12[:, 1, :], l12[:, 0, :], ALU.subtract))
            dve.tensor_copy(l12[:, 0, :], first_e[:, 0, :]).then_inc(ed_ready, 1)
            dve.wait_ge(ee_ready, 1)
            link(dve.tensor_scalar(slot[:, 0, :], wts[:, 1, :], 1.0, None, ALU.add))
            link(dve.reciprocal(wts[:, 0, :], slot[:, 0, :]))
            link(dve.tensor_tensor(wts[:, 1, :], wts[:, 1, :], wts[:, 0, :], ALU.mult))
            dve.wait_ge(cnt_done, 1)
            for h in range(2):
                ins = dve.tensor_copy(by_et(cnt)[:, :, h * NT // 2:(h + 1) * NT // 2],
                                      bank[2 + h][:, :].rearrange("p (t e) -> p e t", e=E))
            link(ins)
            link(dve.tensor_tensor_scan(run, seg, cnt, 0.0, ALU.mult, ALU.add))
            link(dve.tensor_copy(ec, by_et(run)[:, :, NT - 1]))
            link(dve.tensor_scalar(eti, ec, 1.0 / P, 0.5 - 0.5 / P, ALU.mult, ALU.add))
            link(dve.tensor_copy(et, eti))
            link(dve.tensor_tensor_scan(ecum, eone, et, 0.0, ALU.mult, ALU.add))
            link(dve.tensor_tensor(ec, ecum, et, ALU.subtract))
            link(dve.tensor_scalar(ebase, ec, float(P), None, ALU.mult))
            link(dve.tensor_tensor(pos, run, cnt, ALU.subtract))
            link(dve.tensor_tensor(by_et(pos), by_et(pos), ebase.unsqueeze(2).to_broadcast([P, E, NT]), ALU.add))
            for h in range(2):
                ins = dve.tensor_tensor(by_te(tmp)[:, h * NT // 2:(h + 1) * NT // 2, :],
                                        pos.rearrange("p (e t) -> p t e", e=E)[:, h * NT // 2:(h + 1) * NT // 2, :],
                                        by_te(bank[h][:, :]), ALU.add)
            link(ins)
            for c, oh in enumerate((oh1, oh2)):
                link(dve.tensor_tensor(oh, oh, tmp, ALU.mult))
                link(dve.tensor_reduce(slot[:, c, :], by_te(oh), AX.X, ALU.add))
            flat = slot.rearrange("p c t -> p (c t)")
            link(dve.tensor_scalar(slot_ti, flat, 1.0 / P, 0.5 / P - 0.5, ALU.mult, ALU.add))
            link(dve.tensor_copy(slot_t, slot_ti))
            link(dve.scalar_tensor_tensor(out=slot_r, in0=slot_t, scalar=-float(P), in1=flat,
                                          op0=ALU.mult, op1=ALU.add))
            c1 = cmpt[0:1, :].rearrange("p (i e) -> p i e", e=E)
            link(dve.tensor_tensor(c1, iota_t[0:1, :].unsqueeze(2).to_broadcast([1, ST, E]),
                                   ecum[0:1, :].unsqueeze(1).to_broadcast([1, ST, E]), ALU.is_ge))
            link(dve.tensor_reduce(tex[0:1, :], c1, AX.X, ALU.add))
            dve.tensor_scalar(texi[0:1, :], tex[0:1, :], float(E - 1), None, ALU.min).then_inc(tex_ready, 1)

            def hots(n, u):
                for j in range(JC):
                    dve.tensor_scalar(oh_r[:, u, j * P:(j + 1) * P], iota_r, slot_r[:, bass.ds(JC * n + j, 1)], None,
                                      ALU.is_equal)
                    ins = dve.tensor_scalar(oh_t[:, u, j * ST:(j + 1) * ST], iota_t, slot_t[:, bass.ds(JC * n + j, 1)],
                                            pair_no[:, bass.ds(JC * n + j, 1)], ALU.is_equal, ALU.mult)
                ins.then_inc(hots_ready, 1)

            for n in range(2):
                hots(n, n)
            with dve.Fori(1, PAIRS // JC // 2) as i:
                for u in range(2):
                    dve.wait_ge(pairs_done, 2 * i + u - 1)
                    hots(2 * i + u, u)
            dve.wait_ge(pairs_done, PAIRS // JC)
            link(dve.scalar_tensor_tensor(out=row, in0=bank[4][:, 0:ST], scalar=0.0, in1=dump,
                                          op0=ALU.is_equal, op1=ALU.mult))
            link(dve.tensor_tensor(row, row, bank[4][:, 0:ST], ALU.add))
            dve.tensor_scalar(to_row, row, -1.0, None, ALU.add).then_inc(rows_known, 1)
            link(dve.tensor_scalar(wrap, bank[4][:, 0:ST], float(N + 1), -float(N), ALU.is_ge, ALU.mult))
            link(dve.tensor_tensor(wrap, wrap, bank[4][:, 0:ST], ALU.add))
            dve.tensor_scalar(from_row, wrap, -1.0, 0.0, ALU.add, ALU.max).then_inc(rows_known, 1)

            def do_hid(i, v, first):
                dve.wait_ge(silu_ready, i + 1)
                if not first:
                    dve.wait_ge(hT_done, i - 1)
                dve.tensor_tensor(hid[:, v, :], silu[:, v, :], bank[2 + v][:, HID:2 * HID], ALU.mult
                                  ).then_inc(hid_ready, 1)

            def copy_hT(i, v, first):
                dve.wait_ge(hT_done, i + 1)
                if not first:
                    dve.wait_ge(y_done, i - 1)
                dve.tensor_copy(hidT[:, v, :], bank[4 + v][:, 0:HID]).then_inc(hT_ready, 1)

            do_hid(0, 0, True)
            copy_hT(0, 0, True)
            do_hid(1, 1, True)
            copy_hT(1, 1, True)
            with dve.Fori(1, ST // 2) as g:
                for v in range(2):
                    do_hid(2 * g + v, v, False)
                    copy_hT(2 * g + v, v, False)

            with dve.Fori(0, NT // GR // 2) as i:
                for u in range(2):
                    dve.wait_ge(res_in[u], 32 * (i + 1))
                    for c, done in enumerate((comb1, comb2)):
                        for k in range(GR):
                            t = bass.ds(GR * (2 * i + u) + k, 1)
                            xt = xm[:, t, :].rearrange("p a d -> p (a d)")
                            if c == 1:
                                dve.wait_ge(comb1, GR * (2 * i + u) + k + 1)
                            dve.scalar_tensor_tensor(out=xt, in0=gat[:, (2 * u + c) * GR + k, :], scalar=wts[:, c, t],
                                                     in1=xt, op0=ALU.mult, op1=ALU.add).then_inc(done, 1)


_INS = ["x", "adj", "L0_gnn_W", "L0_gnn_b_W", "L0_gnn_a_vec", "L0_gnn_b_a", "L0_ffn_gate_w", "L0_ffn_gate_b",
        "L0_ffn_w1", "L0_ffn_w2", "L0_ffn_w3"]


def kernel(**inputs):
    import numpy as np
    import concourse.bacc as bacc
    from concourse.bass_utils import run_bass_kernel_spmd

    nc = bacc.Bacc("TRN2", target_bir_lowering=False, num_devices=1, dynamic_dma_scratch_size=8192)
    arrays, args = {}, []
    for name in _INS:
        a = np.ascontiguousarray(inputs[name])
        arrays[f"in_{name}"] = a
        args.append(nc.dram_tensor(f"in_{name}", a.shape, mybir.dt.from_np(a.dtype), kind="ExternalInput").ap())
    out = nc.dram_tensor("out", inputs["x"].shape, F32, kind="ExternalOutput").ap()
    graph_moe_layer(nc, *args, out)
    r = run_bass_kernel_spmd(nc, [arrays], core_ids=[0])
    return r.results[0]["out"]
```
